# Optimizing a Trainium2 kernel written in Bass

```python
import numpy as np
import jax
import jax.numpy as jnp

def _softmax(x, axis=-1):
    return jax.nn.softmax(x, axis=axis)

def _gelu(x):
    return jax.nn.gelu(x, approximate=True)

def _silu(x):
    return jax.nn.silu(x)

def _sigmoid(x):
    return jax.nn.sigmoid(x)

def _layernorm(x, axis=-1, eps=1e-05):
    m = jnp.mean(x, axis=axis, keepdims=True)
    v = jnp.var(x, axis=axis, keepdims=True)
    return (x - m) / jnp.sqrt(v + eps)

def _scatter_add(tgt, idx, src, axis=0):
    return tgt.at[idx].add(src)

def _segment_sum(src, seg, n):
    return jax.ops.segment_sum(src, seg, n)
kernel_name = 'mk_perceiver_d1_seqx_r4_ac92ac'

def setup_inputs(seed: int=0):
    np.random.seed(seed)
    _w = jnp.asarray

    def _rec_inputs():
        import jax
        import jax.numpy as jnp
        _rk = jax.random.key(seed)
        x = -0.0002928 + 1 * jax.random.normal(jax.random.fold_in(_rk, 1), (8, 64, 256), jnp.float32)
        _lenS = 64 - jax.random.randint(jax.random.fold_in(_rk, 7), (8,), 0, max(1, 64 // 4) + 1, jnp.int32)
        _lenS2 = 1601 - jax.random.randint(jax.random.fold_in(_rk, 8), (8,), 0, max(1, 1601 // 4) + 1, jnp.int32)
        _ctx_1024P = jax.random.normal(jax.random.fold_in(_rk, 11), (8, 16, 256), jnp.float32)
        _ctx_1024c = jax.random.dirichlet(jax.random.fold_in(_rk, 511), 0.3 * jnp.ones((16,), jnp.float32), (8, 1601))
        _ctx_1024t = jnp.einsum('bsk,bkd->bsd', _ctx_1024c, _ctx_1024P)
        _ctx_1024t = _ctx_1024t * jax.lax.rsqrt(jnp.mean(jnp.square(_ctx_1024t)) + 1e-12) * 0.953939
        ctx_1024 = -1.39393e-06 + 0.999914 * (_ctx_1024t + 0.3 * jax.random.normal(jax.random.fold_in(_rk, 611), (8, 1601, 256), jnp.float32))
        return (x, ctx_1024)
    x, ctx_1024 = _rec_inputs()

    def _L0_xattn_setup():
        import jax, jax.numpy as jnp
        import numpy as np
        import math
        D_MODEL = 256
        HEADS = 16
        DK = 64
        DV = 64
        key = jax.random.key(seed)
        ks = jax.random.split(key, 8)
        N, QL, KL = (2, 512, 512)
        s = 1.0 / math.sqrt(D_MODEL)
        return {'Q': jax.random.normal(ks[0], (N, QL, D_MODEL), jnp.float32), 'K': jax.random.normal(ks[1], (N, KL, D_MODEL), jnp.float32), 'V': jax.random.normal(ks[2], (N, KL, D_MODEL), jnp.float32), 'WQ': jax.random.normal(ks[3], (D_MODEL, HEADS * DK), jnp.float32) * s, 'WK': jax.random.normal(ks[4], (D_MODEL, HEADS * DK), jnp.float32) * s, 'WV': jax.random.normal(ks[5], (D_MODEL, HEADS * DV), jnp.float32) * s, 'WO': jax.random.normal(ks[6], (HEADS * DV, D_MODEL), jnp.float32) * (1.0 / math.sqrt(HEADS * DV)), 'bO': jnp.zeros((D_MODEL,), jnp.float32)}
    _L0_xattn_all = _L0_xattn_setup()
    _L0_xattn_in = {k: v for k, v in _L0_xattn_all.items() if k in ('WQ', 'WK', 'WV', 'WO', 'bO')}
    del _L0_xattn_all

    def _L0_attn_setup():
        import jax, jax.numpy as jnp
        import numpy as np
        B, S, D = (2, 512, 256)
        H, P = (16, 64)
        NUM_OUT = 256
        key = jax.random.key(seed)
        ks = jax.random.split(key, 9)
        sc = 0.05
        return {'x': jax.random.normal(ks[0], (B, S, D), jnp.float32), 'q_w': jax.random.normal(ks[1], (H, P, D), jnp.float32) * sc, 'q_b': jax.random.normal(ks[2], (H, 1, P), jnp.float32) * sc, 'k_w': jax.random.normal(ks[3], (H, P, D), jnp.float32) * sc, 'k_b': jax.random.normal(ks[4], (H, 1, P), jnp.float32) * sc, 'v_w': jax.random.normal(ks[5], (H, P, D), jnp.float32) * sc, 'v_b': jax.random.normal(ks[6], (H, 1, P), jnp.float32) * sc, 'l_w': jax.random.normal(ks[7], (NUM_OUT, P * H), jnp.float32) * sc, 'l_b': jax.random.normal(ks[8], (1, NUM_OUT), jnp.float32) * sc}
    _L0_attn_all = _L0_attn_setup()
    _L0_attn_in = {k: v for k, v in _L0_attn_all.items() if k in ('q_w', 'q_b', 'k_w', 'k_b', 'v_w', 'v_b', 'l_w', 'l_b')}
    del _L0_attn_all

    def _L0_ffn_setup():
        import jax, jax.numpy as jnp
        import numpy as np
        DIM = 256
        HIDDEN = 768
        SCALE = 1.0 / 127.0

        def _dequant(w_int, dtype):
            return w_int.astype(dtype) * jnp.asarray(SCALE, dtype)
        key = jax.random.key(seed)
        k_x, k_g, k_u, k_d = jax.random.split(key, 4)
        x = jax.random.normal(k_x, (4, 512, DIM), dtype=jnp.float32)
        w_gate = jax.random.randint(k_g, (HIDDEN, DIM), -127, 128, dtype=jnp.int32)
        w_up = jax.random.randint(k_u, (HIDDEN, DIM), -127, 128, dtype=jnp.int32)
        w_down = jax.random.randint(k_d, (DIM, HIDDEN), -127, 128, dtype=jnp.int32)
        return {'x': x, 'w_gate': w_gate, 'w_up': w_up, 'w_down': w_down}
    _L0_ffn_all = _L0_ffn_setup()
    _L0_ffn_in = {k: v for k, v in _L0_ffn_all.items() if k in ('w_gate', 'w_up', 'w_down')}
    del _L0_ffn_all
    return {'x': x, 'ctx_1024': ctx_1024, 'L0_xattn_WQ': _L0_xattn_in['WQ'], 'L0_xattn_WK': _L0_xattn_in['WK'], 'L0_xattn_WV': _L0_xattn_in['WV'], 'L0_xattn_WO': _L0_xattn_in['WO'], 'L0_xattn_bO': _L0_xattn_in['bO'], 'L0_attn_q_w': _L0_attn_in['q_w'], 'L0_attn_q_b': _L0_attn_in['q_b'], 'L0_attn_k_w': _L0_attn_in['k_w'], 'L0_attn_k_b': _L0_attn_in['k_b'], 'L0_attn_v_w': _L0_attn_in['v_w'], 'L0_attn_v_b': _L0_attn_in['v_b'], 'L0_attn_l_w': _L0_attn_in['l_w'], 'L0_attn_l_b': _L0_attn_in['l_b'], 'L0_ffn_w_gate': _L0_ffn_in['w_gate'], 'L0_ffn_w_up': _L0_ffn_in['w_up'], 'L0_ffn_w_down': _L0_ffn_in['w_down']}

def reference(x, ctx_1024, L0_xattn_WQ, L0_xattn_WK, L0_xattn_WV, L0_xattn_WO, L0_xattn_bO, L0_attn_q_w, L0_attn_q_b, L0_attn_k_w, L0_attn_k_b, L0_attn_v_w, L0_attn_v_b, L0_attn_l_w, L0_attn_l_b, L0_ffn_w_gate, L0_ffn_w_up, L0_ffn_w_down):
    import jax
    import jax.numpy as jnp

    def _L0_xattn_ref(Q, K, V, WQ, WK, WV, WO, bO):
        import jax, jax.numpy as jnp
        import numpy as np
        import math
        D_MODEL = 256
        HEADS = 16
        DK = 64
        DV = 64
        N, ql, _ = Q.shape
        kl = K.shape[1]
        q = (Q @ WQ).reshape(N, ql, HEADS, DK)
        k = (K @ WK).reshape(N, kl, HEADS, DK)
        v = (V @ WV).reshape(N, kl, HEADS, DV)
        compat = jnp.einsum('nqhk,nlhk->nhql', q, k) / math.sqrt(DK)
        weights = jax.nn.softmax(compat, axis=3)
        attn = jnp.einsum('nhqk,nkhv->nqhv', weights, v).reshape(N, ql, HEADS * DV)
        return attn @ WO + bO

    def _L0_attn_ref(x, q_w, q_b, k_w, k_b, v_w, v_b, l_w, l_b):
        import jax, jax.numpy as jnp
        import numpy as np
        B, S, D = (2, 512, 256)
        H, P = (16, 64)
        NUM_OUT = 256
        q = jnp.einsum('bsd,hpd->bhsp', x, q_w) + q_b
        k = jnp.einsum('bsd,hpd->bhsp', x, k_w) + k_b
        v = jnp.einsum('bsd,hpd->bhsp', x, v_w) + v_b
        scores = jnp.einsum('bhqp,bhkp->bhqk', q, k) / jnp.sqrt(jnp.float32(P))
        attn = jax.nn.softmax(scores, axis=2)
        ctx = jnp.einsum('bhqk,bhkp->bqhp', attn, v)
        concat = ctx.reshape(ctx.shape[0], ctx.shape[1], H * P)
        out = concat @ l_w.T + l_b
        return out

    def _L0_ffn_ref(x, w_gate, w_up, w_down):
        import jax, jax.numpy as jnp
        import numpy as np
        DIM = 256
        HIDDEN = 768
        SCALE = 1.0 / 127.0

        def _dequant(w_int, dtype):
            return w_int.astype(dtype) * jnp.asarray(SCALE, dtype)
        wg = _dequant(w_gate, x.dtype)
        wu = _dequant(w_up, x.dtype)
        wd = _dequant(w_down, x.dtype)
        gate = jnp.einsum('bsd,hd->bsh', x, wg)
        up = jnp.einsum('bsd,hd->bsh', x, wu)
        h = jax.nn.silu(gate) * up
        return jnp.einsum('bsh,dh->bsd', h, wd)
    x = x + _L0_xattn_ref(_layernorm(x, axis=-1), ctx_1024, ctx_1024, L0_xattn_WQ, L0_xattn_WK, L0_xattn_WV, L0_xattn_WO, L0_xattn_bO)
    x = x + _L0_attn_ref(_layernorm(x, axis=-1), L0_attn_q_w, L0_attn_q_b, L0_attn_k_w, L0_attn_k_b, L0_attn_v_w, L0_attn_v_b, L0_attn_l_w, L0_attn_l_b)
    x = x + _L0_ffn_ref(_layernorm(x, axis=-1), L0_ffn_w_gate, L0_ffn_w_up, L0_ffn_w_down)
    return x

_drawn_inputs = setup_inputs


def setup_inputs(seed=0):
    import zlib

    import numpy as np

    out = dict(_drawn_inputs(seed))
    spreads = {'L0_xattn_bO': (0.0, 0.1)}
    factors = {}
    for name, (base, spread) in spreads.items():
        noise = np.random.default_rng([zlib.crc32(name.encode()), seed]).standard_normal(out[name].shape)
        drawn = base * np.exp(spread * noise) if base else spread * noise
        out[name] = jnp.asarray(drawn.astype(out[name].dtype))
    for name, factor in factors.items():
        out[name] = (out[name] * factor).astype(out[name].dtype)
    return out
```

```python
from contextlib import ExitStack

import concourse.bass as bass
from concourse import mybir

F32 = mybir.dt.float32
F32R = mybir.dt.float32r
I32 = mybir.dt.int32
ALU = mybir.AluOpType
ACT = mybir.ActivationFunctionType
AX = mybir.AxisListType

P = 128
EPS = 1e-5
SBUF_START = 16512


def perceiver_layer(nc, x, ctx, WQ, WK, WV, WO, bO, q_w, q_b, k_w, k_b, v_w, v_b, l_w, l_b,
                    w_gate, w_up, w_down, out):
    NB, SQ, D = x.shape
    SL = ctx.shape[1]
    HD = WQ.shape[1]
    KD = D // P
    NT = HD // P
    DH = P // 2
    TOK = NB * SQ
    NI = TOK // P
    G = NB * NT
    JF = SL // P
    JR = SL - JF * P
    NJ = JF + 1
    NC = 4
    CW = (SL - 1) // NC
    SLP = NC * CW + 2
    HID = w_gate.shape[0]
    NM = HID // P
    SCALE = float(DH) ** -0.5
    assert NC * CW + 1 == SL and CW % 2 == 0 and SQ == DH and 0 < JR < P and NT == 8

    GROUPS = [(0, 4), (4, 8), (8, 12), (12, NJ)]
    CTG = [(0, 2), (2, 4), (4, 6), (6, 8), (8, 10), (10, 11), (11, 12), (12, NJ)]
    NG, NCT = len(GROUPS), len(CTG)
    RING = NT * NG + NCT
    CT_STEP = NT - 2

    place = [SBUF_START]

    def sb(name, shape, dt=F32, at=None):
        n = 4
        for s in shape[1:]:
            n *= s
        n = (n + 31) // 32 * 32
        if at is None:
            at = place[0]
            place[0] += n
        return nc.alloc_sbuf_tensor_at(name, shape, dt, offset=at)

    ident = sb("ident", [P, P])
    xs = sb("xs", [P, NI, D])
    bo_row = sb("bo_row", [P, D])
    lb_row = sb("lb_row", [P, D])
    vb_row = sb("vb_row", [P, HD])
    qb_col = sb("qb_col", [P, NT])
    kb_col = sb("kb_col", [P, NT])
    stats = sb("stats", [P, NI, 6])
    meanvar = sb("meanvar", [P, NI, 2])
    veps = sb("veps", [P, NI])
    std = sb("std", [P, NI])
    rstd = sb("rstd", [P, NI])
    rowmax = sb("rowmax", [P, 2])
    negmax = sb("negmax", [P, 2])
    expsum = sb("expsum", [P, 2])
    rowsum = sb("rowsum", [P, 2])
    rinv = sb("rinv", [P, 2])
    colmax = sb("colmax", [P, 2 * NT])
    colsum = sb("colsum", [P, 2 * NT])
    colinv = sb("colinv", [P, 2 * NT])
    xn = sb("xn", [P, NI, D])
    xnT = sb("xnT", [P, KD, TOK])
    heads_at = place[0]
    headsT = sb("headsT", [P, NT, TOK])
    WQs = sb("WQs", [P, KD, HD], at=heads_at)
    WKs = sb("WKs", [P, KD, HD], at=heads_at + 4 * KD * HD)
    WVs = sb("WVs", [P, KD, HD])
    wo_at = place[0]
    WKT = sb("WKT", [P, NT, D])
    WOs = sb("WOs", [P, NT, D], at=wo_at)
    qbd_at = place[0]
    qbd = sb("qbd", [P, NT, NB, P])
    work_at = place[0]
    ctxT = sb("ctxT", [P, 2, KD, SLP], F32R)
    probs = sb("probs", [P, SL])
    probsT = sb("probsT", [P, 2, NJ, P], F32R)
    qp = sb("qp", [P, 2, KD, P], F32R)
    o_lo = sb("o_lo", [P, D])
    o_sb = sb("o_sb", [P, D])
    oT = sb("oT", [P, KD, P])
    raw_at = place[0]
    raw = sb("raw", [P, NJ, D])
    ctxs_at = place[0]
    ctxs = sb("ctxs", [P, 2, NJ, 2, D], F32R)
    assert place[0] <= nc.sbuf_usable_end, place[0]

    nat = [sb(f"nat{n}", [P, NT, D] if n < 3 else [P, KD, HD], at=raw_at + n * 4 * HD * KD) for n in range(4)]
    assert raw_at + 4 * 4 * HD * KD <= ctxs_at + 4 * NJ * 2 * D
    wT = [sb(f"wT{n}", [P, KD, HD] if n < 3 else [P, NT, D], at=qbd_at + n * 4 * HD * KD) for n in range(4)]
    FB = 4 * NM * D
    fint = [sb(f"fint{n}", [P, NM, D] if n < 2 else [P, KD, HID], I32, at=raw_at + n * FB) for n in range(3)]
    fnat = [f[:].bitcast(F32) for f in fint]
    fT = [sb(f"fT{n}", [P, KD, HID] if n < 2 else [P, NM, D], at=raw_at + (3 + n) * FB) for n in range(3)]
    q2 = sb("q2", [P, NT, NB, P], at=work_at)
    kT2 = sb("kT2", [P, NT, TOK], at=work_at + 4 * NT * NB * P)
    assert work_at + 4 * NT * (NB * P + TOK) <= raw_at
    s1_at = ctxs_at + 4 * NJ * 2 * D
    v2 = sb("v2", [P, NI, HD], at=s1_at)
    att = sb("att", [P, 2, 2 * NT, SQ], at=s1_at + 4 * NI * HD)
    assert s1_at + 4 * (NI * HD + 4 * NT * SQ) <= place[0]
    hT = sb("hT", [P, NM, TOK], at=qbd_at)
    eg = sb("eg", [P, 2, TOK], at=qbd_at + 4 * NM * TOK)
    sg = sb("sg", [P, 2, TOK], at=qbd_at + 4 * (NM + 2) * TOK)

    x_tok = x.rearrange("b q d -> (b q) d").rearrange("(i p) d -> p i d", p=P)
    out_tok = out.rearrange("b q d -> (b q) d").rearrange("(i p) d -> p i d", p=P)

    def row(v, n):
        return v.rearrange("(a n) -> a n", a=1).broadcast_to([P, n])

    with ExitStack() as es:
        ps = es.enter_context(nc.psum_tensor("ps", [P, 8, 512], F32))
        SC, TP, ACC, MISC = 0, 4, 6, 7

        def sem(name):
            return es.enter_context(nc.semaphore(name))

        x_loaded, wq_loaded, wk_loaded, wv_loaded = sem("x_loaded"), sem("wq_loaded"), sem("wk_loaded"), sem("wv_loaded")
        raw_loaded, rows_loaded, wo_loaded, nat_loaded, f_loaded = (
            sem("raw_loaded"), sem("rows_loaded"), sem("wo_loaded"), sem("nat_loaded"), sem("f_loaded"))
        ident_zeroed, ident_ready, pads_zeroed, qbd_zeroed, q2_zeroed = (
            sem("ident_zeroed"), sem("ident_ready"), sem("pads_zeroed"), sem("qbd_zeroed"), sem("q2_zeroed"))
        ln_stats, ln_mv, ln_veps, ln_std, ln_rstd, ln_done = (
            sem("ln_stats"), sem("ln_mv"), sem("ln_veps"), sem("ln_std"), sem("ln_rstd"), sem("ln_done"))
        xnT_filled, xnT_lo_copied, xnT_hi_copied = sem("xnT_filled"), sem("xnT_lo_copied"), sem("xnT_hi_copied")
        wkT_filled, wkT_copied, q_filled, q_low, q_high = (
            sem("wkT_filled"), sem("wkT_copied"), sem("q_filled"), sem("q_low"), sem("q_high"))
        ring_filled, ring_hi, ring_freed = sem("ring_filled"), sem("ring_hi"), sem("ring_freed")
        scores_filled, row_max, neg_max, exp_done, sum_done, rinv_ready = (
            sem("scores_filled"), sem("row_max"), sem("neg_max"), sem("exp_done"), sem("sum_done"), sem("rinv_ready"))
        av_filled, olo_ready, o_ready = sem("av_filled"), sem("olo_ready"), sem("o_ready")
        ot_filled, ot_copied, vp_filled, vp_low, vp_high = (
            sem("ot_filled"), sem("ot_copied"), sem("vp_filled"), sem("vp_low"), sem("vp_high"))
        qp_filled, qp_hi, qp_ready = sem("qp_filled"), sem("qp_hi"), sem("qp_ready")
        ctx_hi, ctx_lo, ctx_ready = sem("ctx_hi"), sem("ctx_lo"), sem("ctx_ready")
        wt_filled, wt_act, wt_dve, f_scaled = sem("wt_filled"), sem("wt_act"), sem("wt_dve"), sem("f_scaled")
        xb_ready, y_filled, x_ready = sem("xb_ready"), sem("y_filled"), sem("x_ready")
        p_filled, p_act, p_dve = sem("p_filled"), sem("p_act"), sem("p_dve")
        s_filled, col_max, s_shifted, s_exp, col_sum, col_inv, att_ready = (
            sem("s_filled"), sem("col_max"), sem("s_shifted"), sem("s_exp"), sem("col_sum"), sem("col_inv"), sem("att_ready"))
        c_filled, c_low, c_high = sem("c_filled"), sem("c_low"), sem("c_high")
        g_filled, g_exp, g_plus, g_rec, g_silu, h_ready = (
            sem("g_filled"), sem("g_exp"), sem("g_plus"), sem("g_rec"), sem("g_silu"), sem("h_ready"))
        stored = sem("stored")

        block = es.enter_context(nc.Block())

        def ct_base(b):
            return 0 if isinstance(b, int) and b == 0 else b * RING - NG

        def t_base(b, t, last):
            return NCT + b * RING + t * NG + (NCT if t > CT_STEP and not last else 0)

        def ring_bank(n):
            return TP + n % 2

        def wt_dest(n):
            if n < 16:
                w, c = wT[n // 4], n % 4
            else:
                w, c = fT[(n - 16) // 3], (n - 16) % 3
            return w[:].rearrange("p a b -> p (a b)")[:, c * 512:(c + 1) * 512]

        def batches(eng, step):
            for t in range(NT):
                step(0, t, True, False)
            with eng.Fori(1, NB - 1) as b:
                for t in range(NT):
                    step(b, t, False, False)
            for t in range(NT):
                step(NB - 1, t, False, True)

        @block.sync
        def _(sp):
            def load_raw(b):
                sp.dma_start(raw[:, 0:JF, :], ctx[b, 0:JF * P, :].rearrange("(p j) d -> p j d", j=JF)
                             ).then_inc(raw_loaded, 16)
                sp.dma_start(raw[0:JR, JF, :], ctx[b, JF * P:SL, :]).then_inc(raw_loaded, 16)

            sp.dma_start(xs[:], x_tok).then_inc(x_loaded, 16)
            sp.dma_start(WQs[:], WQ.rearrange("(k p) n -> p k n", p=P)).then_inc(wq_loaded, 16)
            load_raw(0)
            sp.dma_start(WVs[:], WV.rearrange("(k p) n -> p k n", p=P)).then_inc(wv_loaded, 16)
            sp.wait_ge(ring_filled, NCT)
            sp.wait_ge(ctx_ready, 1)
            load_raw(1)
            with sp.Fori(2, NB) as b:
                sp.wait_ge(ring_filled, ct_base(b - 1) + NCT)
                sp.wait_ge(ctx_ready, b)
                load_raw(b)
            sp.wait_ge(ring_filled, ct_base(NB - 1) + NCT)
            sp.wait_ge(ctx_ready, NB)
            sp.wait_ge(av_filled, NT * (NB - 1))
            for n, w in enumerate((q_w, k_w, v_w)):
                sp.dma_start(nat[n][:], w.rearrange("h p d -> (h p) d").rearrange("(r p) d -> p r d", p=P)
                             ).then_inc(nat_loaded, 16)
            sp.dma_start(nat[3][:], l_w.rearrange("(k p) n -> p k n", p=P)).then_inc(nat_loaded, 16)
            sp.wait_ge(qp_filled, G)
            sp.dma_start(WOs[:], WO.rearrange("(t p) n -> p t n", p=P)).then_inc(wo_loaded, 16)
            sp.wait_ge(wt_filled, 16)
            for n, w in enumerate((w_gate, w_up, w_down)):
                sp.dma_start(fint[n][:], w.rearrange("(r p) d -> p r d", p=P)).then_inc(f_loaded, 16)
            for i in range(NI):
                sp.wait_ge(x_ready, 2 * NI + i + 1)
                sp.dma_start(out_tok[:, i, :], xs[:, i, :]).then_inc(stored, 16)
            sp.wait_ge(stored, 16 * NI)

        @block.gpsimd
        def _(pool):
            pool.memset(ident[:], 0.0).then_inc(ident_zeroed, 1)
            pool.wait_ge(ident_zeroed, 1)
            pool.affine_select(out=ident[:], in_=ident[:], compare_op=ALU.not_equal, fill=1.0, base=0,
                               pattern=[[-1, P]], channel_multiplier=1).then_inc(ident_ready, 1)
            pool.memset(ctxT[:, :, :, SL:SLP].bitcast(F32), 0.0).then_inc(pads_zeroed, 1)
            for half in range(2):
                lo, hi = half * DH, half * DH + DH
                if half:
                    pool.wait_ge(qbd_zeroed, 1)
                else:
                    pool.wait_ge(pads_zeroed, 1)
                pool.memset(qbd[lo:hi, :, :, DH - lo:P - lo], 0.0).then_inc(qbd_zeroed, 1)

            def split(b):
                pool.wait_ge(raw_loaded, 32 * b + 32)
                if isinstance(b, int) and b == 0:
                    pool.wait_ge(qbd_zeroed, 2)
                else:
                    pool.wait_ge(ctx_ready, b)
                parts = ((0, JF, P), (JF, NJ, JR))
                for n, (j0, j1, rows) in enumerate(parts):
                    if n:
                        pool.wait_ge(ctx_hi, 2 * b + 1)
                    pool.tensor_copy(ctxs[0:rows, b % 2, j0:j1, 0, :], raw[0:rows, j0:j1, :]).then_inc(ctx_hi, 1)
                pool.wait_ge(ctx_hi, 2 * b + 2)
                for n, (j0, j1, rows) in enumerate(parts):
                    if n:
                        pool.wait_ge(ctx_lo, b + 1)
                    pool.tensor_tensor(ctxs[0:rows, b % 2, j0:j1, 1, :], raw[0:rows, j0:j1, :],
                                       ctxs[0:rows, b % 2, j0:j1, 0, :].bitcast(F32), ALU.subtract
                                       ).then_inc(ctx_ready if n else ctx_lo, 1)

            split(0)
            split(1)
            with pool.Fori(2, NB) as b:
                pool.wait_ge(av_filled, NT * (b - 1))
                split(b)
            pool.wait_ge(vp_low, G)
            pool.wait_ge(vp_high, G)
            for half in range(2):
                lo, hi = half * DH, half * DH + DH
                if half:
                    pool.wait_ge(q2_zeroed, 1)
                else:
                    pool.wait_ge(ctx_ready, NB)
                pool.memset(q2[lo:hi, :, :, DH - lo:P - lo], 0.0).then_inc(q2_zeroed, 1)
            pool.wait_ge(q2_zeroed, 2)
            pool.wait_ge(f_loaded, 48)
            for n in range(3):
                pool.tensor_scalar(fnat[n], fint[n][:], 1.0 / 127.0, None, ALU.mult).then_inc(f_scaled, 1)

        @block.scalar
        def _(act):
            act.dma_start(WKs[:], WK.rearrange("(k p) n -> p k n", p=P)).then_inc(wk_loaded, 16)
            act.dma_start(bo_row[:], row(bO, D)).then_inc(rows_loaded, 16)
            act.dma_start(lb_row[:], row(l_b.rearrange("a n -> (a n)"), D)).then_inc(rows_loaded, 16)
            act.dma_start(vb_row[:], row(v_b.rearrange("h a p -> (h a p)"), HD)).then_inc(rows_loaded, 16)
            with nc.allow_non_contiguous_dma("one column per tile of two heads"):
                act.dma_start(qb_col[:], q_b.rearrange("(t h) a p -> (h a p) t", h=2)).then_inc(rows_loaded, 16)
                act.dma_start(kb_col[:], k_b.rearrange("(t h) a p -> (h a p) t", h=2)).then_inc(rows_loaded, 16)

            def ln_sqrt(n):
                act.wait_ge(ln_veps, n + 1)
                act.activation(std[:], veps[:], ACT.Sqrt).then_inc(ln_std, 1)

            def xnT_copy(n):
                act.wait_ge(xnT_filled, 2 * n + 1)
                act.activation(xnT[:, 0, :], ps[:, TP, :], ACT.Copy).then_inc(xnT_lo_copied, 1)

            ln_sqrt(0)
            for c in range(4):
                act.wait_ge(wkT_filled, c + 1)
                act.activation(WKT[:, 2 * c:2 * c + 2, :].rearrange("p t d -> p (t d)"), ps[:, SC + c, :], ACT.Copy
                               ).then_inc(wkT_copied, 1)
            xnT_copy(0)
            act.wait_ge(qbd_zeroed, 2)
            for t in range(NT):
                act.wait_ge(q_filled, t + 1)
                act.activation(qbd[0:DH, t, :, 0:DH], ps[0:DH, SC + t % 4, :].rearrange("p (b q) -> p b q", q=SQ),
                               ACT.Copy).then_inc(q_low, 1)

            def ct_hi(b, i):
                j0, j1 = CTG[i]
                w = (j1 - j0) * P if j1 < NJ else JR
                act.wait_ge(ring_filled, ct_base(b) + i + 1)
                src = ps[:, ring_bank(i), :].rearrange("p (k n) -> p k n", k=KD)[:, :, 0:w]
                act.activation(ctxT[:, 0, :, j0 * P:j0 * P + w], src, ACT.Copy).then_inc(ring_hi, 1)

            def t_hi(b, t, i, last):
                j0, j1 = GROUPS[i]
                rows = P if j1 < NJ else JR
                act.wait_ge(ring_filled, t_base(b, t, last) + i + 1)
                act.activation(probsT[0:rows, 0, j0:j1, :].rearrange("p j n -> p (j n)"),
                               ps[0:rows, ring_bank(i), 0:(j1 - j0) * P], ACT.Copy).then_inc(ring_hi, 1)

            def qp_split_hi(g):
                act.wait_ge(qp_filled, g + 1)
                act.activation(qp[:, 0, :, :].rearrange("p k n -> p (k n)"), ps[:, MISC, 0:D], ACT.Copy
                               ).then_inc(qp_hi, 1)

            def exps(g, par):
                act.wait_ge(neg_max, g + 1)
                act.activation(probs[:, 0:NC * CW].rearrange("p (c n) -> p c n", c=NC), ps[:, SC:SC + NC, 0:CW],
                               ACT.Exp, bias=negmax[:, par:par + 1], scale=SCALE, accum_out=expsum[:, par:par + 1])
                act.activation(probs[:, SL - 1:SL], ps[:, SC + NC - 1, CW:CW + 1], ACT.Exp,
                               bias=negmax[:, par:par + 1], scale=SCALE).then_inc(exp_done, 1)

            def o_scale_lo(g, par):
                act.wait_ge(av_filled, g + 1)
                act.wait_ge(rinv_ready, g + 1)
                act.wait_ge(o_ready, g)
                act.activation(o_lo[:], ps[:, ACC, D:2 * D], ACT.Copy, scale=rinv[:, par:par + 1]
                               ).then_inc(olo_ready, 1)

            def ot_copy(g):
                act.wait_ge(ot_filled, g + 1)
                act.activation(oT[:].rearrange("p k n -> p (k n)"), ps[:, MISC, 0:D], ACT.Copy).then_inc(ot_copied, 1)

            def heads_low(b, t, g):
                act.wait_ge(vp_filled, g + 1)
                act.activation(headsT[0:DH, t, bass.ds(b * SQ, SQ)], ps[0:DH, MISC, 0:DH], ACT.Copy).then_inc(vp_low, 1)

            for i in range(NCT):
                ct_hi(0, i)
            qp_split_hi(0)
            exps(0, 0)
            qp_split_hi(1)

            def step(b, t, first, last):
                g = b * NT + t
                before = not (first and t == 0)
                pb, pt = (b, t - 1) if t else (b - 1, NT - 1)
                if before:
                    o_scale_lo(g - 1, (t + 1) % 2)
                t_hi(b, t, 0, last)
                t_hi(b, t, 1, last)
                if before:
                    ot_copy(g - 1)
                t_hi(b, t, 2, last)
                t_hi(b, t, 3, last)
                if before:
                    heads_low(pb, pt, g - 1)
                ct = t == CT_STEP and not last
                for i in range(2 if ct else 0):
                    ct_hi(b + 1, i)
                if not (last and t == NT - 1):
                    exps(g + 1, (t + 1) % 2)
                if not (last and t >= NT - 2):
                    qp_split_hi(g + 2)
                for i in range(2, NCT if ct else 0):
                    ct_hi(b + 1, i)

            batches(act, step)
            o_scale_lo(G - 1, (NT - 1) % 2)
            ot_copy(G - 1)
            heads_low(NB - 1, NT - 1, G - 1)

            def wt_copy(n, dst):
                act.wait_ge(wt_filled, n + 1)
                act.activation(dst, ps[:, n % 8, :], ACT.Copy).then_inc(wt_act, 1)

            for n in range(0, 16, 2):
                wt_copy(n, wt_dest(n))
            ln_sqrt(1)
            xnT_copy(1)
            for n in range(16, 25, 2):
                wt_copy(n, wt_dest(n))
            act.wait_ge(q2_zeroed, 2)
            for t in range(NT):
                act.wait_ge(p_filled, t + 1)
                act.activation(q2[0:DH, t, :, 0:DH], ps[0:DH, t % 4, :].rearrange("p (b q) -> p b q", q=SQ),
                               ACT.Identity, bias=qb_col[0:DH, t:t + 1]).then_inc(p_act, 1)
            for t in range(NT):
                act.wait_ge(p_filled, NT + t + 1)
                act.activation(kT2[:, t, :], ps[:, t % 4, :], ACT.Identity, bias=kb_col[:, t:t + 1]
                               ).then_inc(p_act, 1)

            def heads2_low(i):
                for c in range(4):
                    act.wait_ge(c_filled, 4 * i + c + 1)
                    b = 2 * i + c // 2
                    t0 = (c % 2) * 4
                    act.activation(headsT[0:DH, t0:t0 + 4, b * SQ:(b + 1) * SQ],
                                   ps[0:DH, 4 + c, :].rearrange("p (t n) -> p t n", n=P)[:, :, 0:DH],
                                   ACT.Copy).then_inc(c_low, 1)

            for i in range(NI):
                act.wait_ge(s_shifted, i + 1)
                act.activation(att[:, i % 2, :, :], att[:, i % 2, :, :], ACT.Exp, scale=SCALE).then_inc(s_exp, 1)
                if i:
                    heads2_low(i - 1)
            heads2_low(NI - 1)
            ln_sqrt(2)
            xnT_copy(2)
            for m in range(NM):
                act.wait_ge(g_filled, 2 * m + 1)
                if m >= 2:
                    act.wait_ge(g_plus, m - 1)
                act.activation(eg[:, m % 2, :], ps[:, 2 * (m % 2), :], ACT.Exp, scale=-1.0).then_inc(g_exp, 1)

        @block.vector
        def _(dve):
            def layer_norm(n, loads, value):
                for i in range(NI):
                    dve.wait_ge(loads, value if n == 0 else value + i + 1)
                    dve.bn_stats(stats[:, i, :], xs[:, i, :]).then_inc(ln_stats, 1)
                for i in range(NI):
                    dve.wait_ge(ln_stats, NI * n + i + 1)
                    dve.bn_aggr(meanvar[:, i, :], stats[:, i, :]).then_inc(ln_mv, 1)
                dve.wait_ge(ln_mv, NI * (n + 1))
                dve.tensor_scalar(veps[:], meanvar[:, :, 1], EPS, None, ALU.add).then_inc(ln_veps, 1)
                dve.wait_ge(ln_std, n + 1)
                dve.reciprocal(rstd[:], std[:]).then_inc(ln_rstd, 1)
                dve.wait_ge(ln_rstd, n + 1)
                for i in range(NI):
                    dve.tensor_scalar(xn[:, i, :], xs[:, i, :], meanvar[:, i, 0:1], rstd[:, i:i + 1],
                                      ALU.subtract, ALU.mult).then_inc(ln_done, 1)

            def xnT_copy(n):
                dve.wait_ge(xnT_filled, 2 * n + 2)
                dve.tensor_copy(xnT[:, 1, :], ps[:, TP + 1, :]).then_inc(xnT_hi_copied, 1)

            layer_norm(0, x_loaded, 16)
            xnT_copy(0)
            dve.wait_ge(qbd_zeroed, 2)
            for t in range(NT):
                dve.wait_ge(q_filled, t + 1)
                dve.tensor_copy(qbd[DH:P, t, :, DH:P], ps[DH:P, SC + t % 4, :].rearrange("p (b q) -> p b q", q=SQ)
                                ).then_inc(q_high, 1)

            def ct_lo(b, i):
                j0, j1 = CTG[i]
                w = (j1 - j0) * P if j1 < NJ else JR
                dve.wait_ge(ring_hi, ct_base(b) + i + 1)
                src = ps[:, ring_bank(i), :].rearrange("p (k n) -> p k n", k=KD)[:, :, 0:w]
                dve.tensor_tensor(ctxT[:, 1, :, j0 * P:j0 * P + w], src,
                                  ctxT[:, 0, :, j0 * P:j0 * P + w].bitcast(F32), ALU.subtract).then_inc(ring_freed, 1)

            def t_lo(b, t, i, last):
                j0, j1 = GROUPS[i]
                rows = P if j1 < NJ else JR
                dve.wait_ge(ring_hi, t_base(b, t, last) + i + 1)
                dve.tensor_tensor(probsT[0:rows, 1, j0:j1, :].rearrange("p j n -> p (j n)"),
                                  ps[0:rows, ring_bank(i), 0:(j1 - j0) * P],
                                  probsT[0:rows, 0, j0:j1, :].rearrange("p j n -> p (j n)").bitcast(F32),
                                  ALU.subtract).then_inc(ring_freed, 1)

            def qp_split_lo(g):
                dve.wait_ge(qp_hi, g + 1)
                dve.tensor_tensor(qp[:, 1, :, :].rearrange("p k n -> p (k n)"), ps[:, MISC, 0:D],
                                  qp[:, 0, :, :].rearrange("p k n -> p (k n)").bitcast(F32), ALU.subtract
                                  ).then_inc(qp_ready, 1)

            def maxima(g, par):
                dve.wait_ge(scores_filled, g + 1)
                dve.tensor_reduce(rowmax[:, par:par + 1], ps[:, SC:SC + NC, 0:CW], AX.XY, ALU.max).then_inc(row_max, 1)
                dve.wait_ge(row_max, g + 1)
                dve.tensor_scalar(negmax[:, par:par + 1], rowmax[:, par:par + 1], ps[:, SC + NC - 1, CW:CW + 1],
                                  -SCALE, ALU.max, ALU.mult).then_inc(neg_max, 1)

            def sums(g, par):
                dve.wait_ge(exp_done, g + 1)
                dve.tensor_tensor(rowsum[:, par:par + 1], expsum[:, par:par + 1], probs[:, SL - 1:SL], ALU.add
                                  ).then_inc(sum_done, 1)
                dve.wait_ge(sum_done, g + 1)
                dve.reciprocal(rinv[:, par:par + 1], rowsum[:, par:par + 1]).then_inc(rinv_ready, 1)

            def o_finish(g, par):
                dve.wait_ge(rinv_ready, g + 1)
                dve.wait_ge(olo_ready, g + 1)
                dve.scalar_tensor_tensor(out=o_sb[:], in0=ps[:, ACC, 0:D], scalar=rinv[:, par:par + 1], in1=o_lo[:],
                                         op0=ALU.mult, op1=ALU.add).then_inc(o_ready, 1)

            def heads_high(b, t, g):
                dve.wait_ge(vp_filled, g + 1)
                dve.tensor_copy(headsT[DH:P, t, bass.ds(b * SQ, SQ)], ps[DH:P, MISC, DH:P]).then_inc(vp_high, 1)

            for i in range(NCT):
                ct_lo(0, i)
            qp_split_lo(0)
            maxima(0, 0)
            sums(0, 0)
            qp_split_lo(1)

            def step(b, t, first, last):
                g = b * NT + t
                before = not (first and t == 0)
                pb, pt = (b, t - 1) if t else (b - 1, NT - 1)
                if before:
                    o_finish(g - 1, (t + 1) % 2)
                for i in range(NG):
                    t_lo(b, t, i, last)
                if before:
                    heads_high(pb, pt, g - 1)
                ct = t == CT_STEP and not last
                if not (last and t == NT - 1):
                    maxima(g + 1, (t + 1) % 2)
                for i in range(2 if ct else 0):
                    ct_lo(b + 1, i)
                if not (last and t == NT - 1):
                    sums(g + 1, (t + 1) % 2)
                if not (last and t >= NT - 2):
                    qp_split_lo(g + 2)
                for i in range(2, NCT if ct else 0):
                    ct_lo(b + 1, i)

            batches(dve, step)
            o_finish(G - 1, (NT - 1) % 2)
            heads_high(NB - 1, NT - 1, G - 1)

            def wt_copy(n, dst):
                dve.wait_ge(wt_filled, n + 1)
                dve.tensor_copy(dst, ps[:, n % 8, :]).then_inc(wt_dve, 1)

            def add_bias(n, bias):
                dve.wait_ge(rows_loaded, 16 * 5)
                for i in range(NI):
                    dve.tensor_tensor(xs[:, i, :], xs[:, i, :], bias[:], ALU.add).then_inc(xb_ready, 1)
                dve.wait_ge(xb_ready, NI * (n + 1))

            def add_y(n):
                for i in range(NI):
                    dve.wait_ge(y_filled, NI * n + i + 1)
                    dve.tensor_tensor(xs[:, i, :], ps[:, i, 0:D], xs[:, i, :], ALU.add).then_inc(x_ready, 1)

            for n in range(1, 16, 2):
                wt_copy(n, wt_dest(n))
            add_bias(0, bo_row)
            add_y(0)
            layer_norm(1, x_ready, 0)
            xnT_copy(1)
            for n in range(17, 25, 2):
                wt_copy(n, wt_dest(n))
            dve.wait_ge(q2_zeroed, 2)
            for t in range(NT):
                dve.wait_ge(p_filled, t + 1)
                dve.tensor_scalar(q2[DH:P, t, :, DH:P], ps[DH:P, t % 4, :].rearrange("p (b q) -> p b q", q=SQ),
                                  qb_col[DH:P, t:t + 1], None, ALU.add).then_inc(p_dve, 1)
            for n in range(2 * NI):
                i, c = n // 2, n % 2
                dve.wait_ge(p_filled, 2 * NT + n + 1)
                dve.tensor_tensor(v2[:, i, c * 512:(c + 1) * 512], ps[:, 4 + n % 4, :],
                                  vb_row[:, c * 512:(c + 1) * 512], ALU.add).then_inc(p_dve, 1)
            add_bias(1, lb_row)

            def soft_shift(i):
                bank = 2 * (i % 2)
                sc = ps[:, bank:bank + 2, :].rearrange("p c (h q) -> p (c h) q", q=SQ)
                dve.wait_ge(s_filled, i + 1)
                dve.tensor_reduce(colmax[:], sc, AX.X, ALU.max).then_inc(col_max, 1)
                dve.wait_ge(col_max, i + 1)
                if i >= 2:
                    dve.wait_ge(c_filled, 4 * (i - 1))
                dve.tensor_tensor(att[:, i % 2, :, :], sc, colmax[:].unsqueeze(2).broadcast_to([P, 2 * NT, SQ]),
                                  ALU.subtract).then_inc(s_shifted, 1)

            def soft_norm(i):
                dve.wait_ge(s_exp, i + 1)
                dve.tensor_reduce(colsum[:], att[:, i % 2, :, :], AX.X, ALU.add).then_inc(col_sum, 1)
                dve.wait_ge(col_sum, i + 1)
                dve.reciprocal(colinv[:], colsum[:]).then_inc(col_inv, 1)
                dve.wait_ge(col_inv, i + 1)
                dve.tensor_tensor(att[:, i % 2, :, :], att[:, i % 2, :, :],
                                  colinv[:].unsqueeze(2).broadcast_to([P, 2 * NT, SQ]), ALU.mult).then_inc(att_ready, 1)

            def heads2_high(i):
                for c in range(4):
                    dve.wait_ge(c_filled, 4 * i + c + 1)
                    b = 2 * i + c // 2
                    t0 = (c % 2) * 4
                    dve.tensor_copy(headsT[DH:P, t0:t0 + 4, b * SQ:(b + 1) * SQ],
                                    ps[DH:P, 4 + c, :].rearrange("p (t n) -> p t n", n=P)[:, :, DH:P]
                                    ).then_inc(c_high, 1)

            for i in range(NI):
                soft_shift(i)
                soft_norm(i)
                if i:
                    heads2_high(i - 1)
            heads2_high(NI - 1)
            add_y(1)
            layer_norm(2, x_ready, NI)
            xnT_copy(2)
            for m in range(NM):
                dve.wait_ge(g_exp, m + 1)
                dve.tensor_scalar(sg[:, m % 2, :], eg[:, m % 2, :], 1.0, None, ALU.add).then_inc(g_plus, 1)
                dve.wait_ge(g_plus, m + 1)
                dve.reciprocal(sg[:, m % 2, :], sg[:, m % 2, :]).then_inc(g_rec, 1)
                dve.wait_ge(g_rec, m + 1)
                dve.tensor_tensor(sg[:, m % 2, :], ps[:, 2 * (m % 2), :], sg[:, m % 2, :], ALU.mult
                                  ).then_inc(g_silu, 1)
                dve.wait_ge(g_silu, m + 1)
                dve.wait_ge(g_filled, 2 * m + 2)
                dve.tensor_tensor(hT[:, m, :], ps[:, 2 * (m % 2) + 1, :], sg[:, m % 2, :], ALU.mult
                                  ).then_inc(h_ready, 1)
            for i in range(NI):
                dve.wait_ge(y_filled, 2 * NI + i + 1)
                dve.tensor_tensor(xs[:, i, :], ps[:, 4 + i, 0:D], xs[:, i, :], ALU.add).then_inc(x_ready, 1)

        @block.tensor
        def _(pe):
            def transpose_xn(n):
                for k in range(KD):
                    for i in range(NI):
                        if k == 0:
                            pe.wait_ge(ln_done, NI * n + i + 1)
                        ins = pe.transpose(ps[:, TP + k, i * P:(i + 1) * P], xn[:, i, k * P:(k + 1) * P], ident[:])
                    ins.then_inc(xnT_filled, 1)

            pe.wait_ge(ident_ready, 1)
            pe.wait_ge(wk_loaded, 16)
            for t in range(NT):
                for k in range(KD):
                    c = (t % 2) * D + k * P
                    ins = pe.transpose(ps[:, SC + t // 2, c:c + P], WKs[:, k, t * P:(t + 1) * P], ident[:])
                if t % 2:
                    ins.then_inc(wkT_filled, 1)
            transpose_xn(0)
            pe.wait_ge(wq_loaded, 16)
            pe.wait_ge(xnT_lo_copied, 1)
            pe.wait_ge(xnT_hi_copied, 1)
            for t in range(NT):
                if t < 4:
                    pe.wait_ge(wkT_copied, t + 1)
                else:
                    pe.wait_ge(q_low, t - 3)
                    pe.wait_ge(q_high, t - 3)
                for k in range(KD):
                    ins = pe.matmul(ps[:, SC + t % 4, :], WQs[:, k, t * P:(t + 1) * P], xnT[:, k, :],
                                    start=(k == 0), stop=(k == KD - 1))
                ins.then_inc(q_filled, 1)

            def ctx_transposes(b, i):
                j0, j1 = CTG[i]
                n = ct_base(b) + i
                if not (isinstance(b, int) and b == 0 and i < 2):
                    pe.wait_ge(ring_freed, n - 1)
                for k in range(KD):
                    for j in range(j0, j1):
                        r = P if j < JF else JR
                        c = k * 2 * P + (j - j0) * P
                        ins = pe.transpose(ps[:, ring_bank(i), c:c + r], raw[0:r, j, k * P:(k + 1) * P],
                                           ident[0:r, 0:r])
                ins.then_inc(ring_filled, 1)

            def probs_transposes(b, t, i, last):
                j0, j1 = GROUPS[i]
                pe.wait_ge(ring_freed, t_base(b, t, last) + i - 1)
                for j in range(j0, j1):
                    r = P if j < JF else JR
                    c = (j - j0) * P
                    ins = pe.transpose(ps[0:r, ring_bank(i), c:c + P], probs[:, j * P:j * P + r], ident[:])
                ins.then_inc(ring_filled, 1)

            def q_by_wk(b, t, g):
                for k in range(KD):
                    ins = pe.matmul(ps[:, MISC, k * P:(k + 1) * P], WKT[:, t, k * P:(k + 1) * P], qbd[:, t, b, :],
                                    start=True, stop=True)
                ins.then_inc(qp_filled, 1)

            def scores_part(part):
                order = [(k, a, c) for k in range(KD) for a, c in ((0, 0), (0, 1), (1, 0))]
                runs = [(r, n) for r in range(len(order)) for n in range(NC)]
                for r, n in runs[6 * part:6 * part + 6]:
                    k, a, c = order[r]
                    w = CW if n < NC - 1 else CW + 2
                    ins = pe.matmul(ps[:, SC + n, 0:w], qp[:, a, k, :], ctxT[:, c, k, n * CW:n * CW + w],
                                    start=(r == 0), stop=(r == len(order) - 1))
                if part == 3:
                    ins.then_inc(scores_filled, 1)

            def o_transposes(g):
                pe.wait_ge(o_ready, g + 1)
                for k in range(KD):
                    ins = pe.transpose(ps[:, MISC, k * P:(k + 1) * P], o_sb[:, k * P:(k + 1) * P], ident[:])
                ins.then_inc(ot_filled, 1)

            def by_wv(t, g):
                pe.wait_ge(ot_copied, g + 1)
                for k in range(KD):
                    ins = pe.matmul(ps[:, MISC, 0:P], WVs[:, k, t * P:(t + 1) * P], oT[:, k, :],
                                    start=(k == 0), stop=(k == KD - 1))
                ins.then_inc(vp_filled, 1)

            pe.wait_ge(raw_loaded, 32)
            for i in range(NCT):
                ctx_transposes(0, i)
            pe.wait_ge(q_low, NT)
            pe.wait_ge(q_high, NT)
            q_by_wk(0, 0, 0)
            pe.wait_ge(pads_zeroed, 1)
            pe.wait_ge(ring_freed, NCT)
            pe.wait_ge(qp_ready, 1)
            for part in range(4):
                scores_part(part)
            q_by_wk(0, 1, 1)
            pe.wait_ge(wv_loaded, 16)

            def step(b, t, first, last):
                g = b * NT + t
                before = not (first and t == 0)
                after = not (last and t == NT - 1)
                ct = t == CT_STEP and not last
                pt = t - 1 if t else NT - 1
                pe.wait_ge(exp_done, g + 1)
                if after:
                    pe.wait_ge(qp_ready, g + 2)
                    if t == NT - 1:
                        pe.wait_ge(ring_freed, ct_base(b + 1) + NCT)
                for i in range(NG):
                    probs_transposes(b, t, i, last)
                    if i == 2 and before:
                        pe.wait_ge(qp_ready, g + 2 if after else g + 1)
                        o_transposes(g - 1)
                    if after:
                        scores_part(i)
                if before:
                    by_wv(pt, g - 1)
                if before:
                    pe.wait_ge(o_ready, g)
                pe.wait_ge(ctx_ready, b + 1)
                cti = 0
                for j in range(NJ):
                    if ct and (j < 2 or j >= 7):
                        if j == 0:
                            pe.wait_ge(raw_loaded, 32 * b + 64)
                        ctx_transposes(b + 1, cti)
                        cti += 1
                    r = P if j < JF else JR
                    for i, (j0, j1) in enumerate(GROUPS):
                        if j == j0:
                            pe.wait_ge(ring_freed, t_base(b, t, last) + i + 1)
                    pe.matmul(ps[:, ACC, :], probsT[0:r, 0, j, :],
                              ctxs[0:r, b % 2, j, :, :].rearrange("p a d -> p (a d)"), start=(j == 0), stop=False)
                    ins = pe.matmul(ps[:, ACC, 0:D], probsT[0:r, 1, j, :], ctxs[0:r, b % 2, j, 0, :],
                                    start=False, stop=(j == NJ - 1))
                    if j == 6 and not (last and t >= NT - 2):
                        nb, nt = (b, t + 2) if t < NT - 2 else (b + 1, t + 2 - NT)
                        if before:
                            pe.wait_ge(vp_low, g)
                            pe.wait_ge(vp_high, g)
                        else:
                            pe.wait_ge(qp_ready, g + 2)
                        q_by_wk(nb, nt, g + 2)
                ins.then_inc(av_filled, 1)
                assert cti == (NCT if ct else 0)

            batches(pe, step)
            pe.wait_ge(vp_low, G - 1)
            pe.wait_ge(vp_high, G - 1)
            o_transposes(G - 1)
            by_wv(NT - 1, G - 1)

            def weight_transposes(n, pieces):
                if n >= 8:
                    s = wt_dve if n % 2 else wt_act
                    pe.wait_ge(s, (n - 8) // 2 + 1)
                for c, piece in enumerate(pieces):
                    ins = pe.transpose(ps[:, n % 8, c * P:(c + 1) * P], piece, ident[:])
                ins.then_inc(wt_filled, 1)

            pe.wait_ge(vp_low, G)
            pe.wait_ge(vp_high, G)
            pe.wait_ge(nat_loaded, 64)
            for n in range(16):
                w, c = n // 4, n % 4
                if w < 3:
                    pieces = [nat[w][:, r % NT, (r // NT) * P:(r // NT + 1) * P] for r in range(4 * c, 4 * c + 4)]
                else:
                    pieces = [nat[w][:, r % KD, (r // KD) * P:(r // KD + 1) * P] for r in range(4 * c, 4 * c + 4)]
                weight_transposes(n, pieces)

            def project(n, src, w, tiles, bank0):
                for i in range(NI):
                    for t in range(tiles):
                        ins = pe.matmul(ps[:, bank0 + i, 0:D], src[:, t, i * P:(i + 1) * P], w[:, t, :],
                                        start=(t == 0), stop=(t == tiles - 1))
                    ins.then_inc(y_filled, 1)

            pe.wait_ge(wo_loaded, 16)
            pe.wait_ge(wt_act, 8)
            pe.wait_ge(wt_dve, 8)
            project(0, headsT, WOs, NT, 0)
            transpose_xn(1)
            pe.wait_ge(xnT_lo_copied, 2)
            pe.wait_ge(xnT_hi_copied, 2)
            pe.wait_ge(f_scaled, 3)
            for n in range(16, 25):
                w, c = (n - 16) // 3, (n - 16) % 3
                if w < 2:
                    pieces = [fnat[w][:, r % NM, (r // NM) * P:(r // NM + 1) * P] for r in range(4 * c, 4 * c + 4)]
                else:
                    pieces = [fnat[w][:, r % KD, (r // KD) * P:(r // KD + 1) * P] for r in range(4 * c, 4 * c + 4)]
                weight_transposes(n, pieces)
            pe.wait_ge(wt_act, 13)
            pe.wait_ge(wt_dve, 12)
            for n in range(2 * NT):
                t = n % NT
                if 4 <= n < NT + 4:
                    pe.wait_ge(p_act, n - 3)
                    pe.wait_ge(p_dve, n - 3)
                elif n >= NT + 4:
                    pe.wait_ge(p_act, n - 3)
                for k in range(KD):
                    ins = pe.matmul(ps[:, n % 4, :], wT[n // NT][:, k, t * P:(t + 1) * P], xnT[:, k, :],
                                    start=(k == 0), stop=(k == KD - 1))
                ins.then_inc(p_filled, 1)
            for n in range(2 * NI):
                i, c = n // 2, n % 2
                if n >= 4:
                    pe.wait_ge(p_dve, NT + n - 3)
                for k in range(KD):
                    ins = pe.matmul(ps[:, 4 + n % 4, :], xnT[:, k, i * P:(i + 1) * P],
                                    wT[2][:, k, c * 512:(c + 1) * 512], start=(k == 0), stop=(k == KD - 1))
                ins.then_inc(p_filled, 1)
            pe.wait_ge(p_act, 2 * NT)

            def self_scores(i):
                if i >= 2:
                    pe.wait_ge(s_shifted, i - 1)
                for t in range(NT):
                    bank = 2 * (i % 2) + t // 4
                    for e in range(2):
                        lo = e * SQ
                        ins = pe.matmul(ps[lo:lo + SQ, bank, (t % 4) * P:(t % 4 + 1) * P],
                                        kT2[:, t, i * P + lo:i * P + lo + SQ], q2[:, t, 2 * i + e, :],
                                        start=True, stop=True)
                ins.then_inc(s_filled, 1)

            def self_heads(i):
                pe.wait_ge(att_ready, i + 1)
                for c in range(4):
                    e, t0 = c // 2, (c % 2) * 4
                    lo = e * SQ
                    if i:
                        pe.wait_ge(c_low, 4 * (i - 1) + c + 1)
                        pe.wait_ge(c_high, 4 * (i - 1) + c + 1)
                    for t in range(t0, t0 + 4):
                        ins = pe.matmul(ps[:, 4 + c, (t - t0) * P:(t - t0 + 1) * P],
                                        v2[lo:lo + SQ, i, t * P:(t + 1) * P],
                                        att[lo:lo + SQ, i % 2, 2 * t:2 * t + 2, :].rearrange("p h q -> p (h q)"),
                                        start=True, stop=True)
                    ins.then_inc(c_filled, 1)

            pe.wait_ge(p_dve, NT + 2 * NI)
            self_scores(0)
            for i in range(NI):
                if i + 1 < NI:
                    self_scores(i + 1)
                self_heads(i)
            pe.wait_ge(c_low, 4 * NI)
            pe.wait_ge(c_high, 4 * NI)
            project(1, headsT, wT[3], NT, 0)
            transpose_xn(2)
            pe.wait_ge(xnT_lo_copied, 3)
            pe.wait_ge(xnT_hi_copied, 3)
            for m in range(NM):
                if m >= 2:
                    pe.wait_ge(h_ready, m - 1)
                for u in range(2):
                    for k in range(KD):
                        ins = pe.matmul(ps[:, 2 * (m % 2) + u, :], fT[u][:, k, m * P:(m + 1) * P], xnT[:, k, :],
                                        start=(k == 0), stop=(k == KD - 1))
                    ins.then_inc(g_filled, 1)
            pe.wait_ge(h_ready, NM)
            project(2, hT, fT[2], NM, 4)


_INS = ['x', 'ctx_1024', 'L0_xattn_WQ', 'L0_xattn_WK', 'L0_xattn_WV', 'L0_xattn_WO', 'L0_xattn_bO',
        'L0_attn_q_w', 'L0_attn_q_b', 'L0_attn_k_w', 'L0_attn_k_b', 'L0_attn_v_w', 'L0_attn_v_b',
        'L0_attn_l_w', 'L0_attn_l_b', 'L0_ffn_w_gate', 'L0_ffn_w_up', 'L0_ffn_w_down']
_OUTS = [((8, 64, 256), 'float32')]


def kernel(**inputs):
    import numpy as _np
    import concourse.bacc as _bacc
    from concourse import mybir as _mybir
    from concourse.bass_utils import run_bass_kernel_spmd as _run

    nc = _bacc.Bacc("TRN2", target_bir_lowering=False, num_devices=1)
    arrays, args = {}, []
    for name in _INS:
        a = _np.ascontiguousarray(inputs[name])
        arrays[f"in_{name}_dram"] = a
        args.append(nc.dram_tensor(f"in_{name}_dram", a.shape, _mybir.dt.from_np(a.dtype), kind="ExternalInput").ap())
    for i, (shape, dtype) in enumerate(_OUTS):
        dt = _mybir.dt.from_np(_np.dtype(dtype))
        args.append(nc.dram_tensor(f"out_{i}_dram", shape, dt, kind="ExternalOutput").ap())
    perceiver_layer(nc, *args)
    r = _run(nc, [arrays], core_ids=[0])
    return r.results[0]["out_0_dram"]
```

```python
from contextlib import ExitStack

import concourse.bass as bass
from concourse import mybir

F32 = mybir.dt.float32
F32R = mybir.dt.float32r
I32 = mybir.dt.int32
ALU = mybir.AluOpType
ACT = mybir.ActivationFunctionType
AX = mybir.AxisListType

P = 128
EPS = 1e-5
SBUF_START = 16512


def perceiver_layer(nc, x, ctx, WQ, WK, WV, WO, bO, q_w, q_b, k_w, k_b, v_w, v_b, l_w, l_b,
                    w_gate, w_up, w_down, out):
    NB, SQ, D = x.shape
    SL = ctx.shape[1]
    HD = WQ.shape[1]
    KD = D // P
    NT = HD // P
    DH = P // 2
    TOK = NB * SQ
    NI = TOK // P
    G = NB * NT
    JF = SL // P
    JR = SL - JF * P
    NJ = JF + 1
    NC = 4
    CW = (SL - 1) // NC
    SLP = NC * CW + 2
    HID = w_gate.shape[0]
    NM = HID // P
    SCALE = float(DH) ** -0.5
    assert NC * CW + 1 == SL and CW % 2 == 0 and SQ == DH and 0 < JR < P and NT == 8

    GROUPS = [(0, 4), (4, 8), (8, 12), (12, NJ)]
    CTG = [(0, 2), (2, 4), (4, 6), (6, 8), (8, 10), (10, 11), (11, 12), (12, NJ)]
    NG, NCT = len(GROUPS), len(CTG)
    RING = NT * NG + NCT
    CT_STEP = NT - 2

    place = [SBUF_START]

    def sb(name, shape, dt=F32, at=None):
        n = 4
        for s in shape[1:]:
            n *= s
        n = (n + 31) // 32 * 32
        if at is None:
            at = place[0]
            place[0] += n
        return nc.alloc_sbuf_tensor_at(name, shape, dt, offset=at)

    ident = sb("ident", [P, P])
    xs = sb("xs", [P, NI, D])
    bo_row = sb("bo_row", [P, D])
    lb_row = sb("lb_row", [P, D])
    vb_row = sb("vb_row", [P, HD])
    qb_col = sb("qb_col", [P, NT])
    kb_col = sb("kb_col", [P, NT])
    stats = sb("stats", [P, NI, 6])
    meanvar = sb("meanvar", [P, NI, 2])
    veps = sb("veps", [P, NI])
    std = sb("std", [P, NI])
    rstd = sb("rstd", [P, NI])
    rowmax = sb("rowmax", [P, 2])
    negmax = sb("negmax", [P, 2])
    expsum = sb("expsum", [P, 2])
    rowsum = sb("rowsum", [P, 2])
    rinv = sb("rinv", [P, 2])
    warm = sb("warm", [P, 8])
    colmax = sb("colmax", [P, 2, 2 * NT])
    colsum = sb("colsum", [P, 2, 2 * NT])
    colinv = sb("colinv", [P, 2, 2 * NT])
    xn = sb("xn", [P, NI, D])
    xnT = sb("xnT", [P, KD, TOK])
    heads_at = place[0]
    headsT = sb("headsT", [P, NT, TOK])
    WQs = sb("WQs", [P, KD, HD], at=heads_at)
    WKs = sb("WKs", [P, KD, HD], at=heads_at + 4 * KD * HD)
    WVs = sb("WVs", [P, KD, HD])
    wo_at = place[0]
    WKT = sb("WKT", [P, NT, D])
    WOs = sb("WOs", [P, NT, D], at=wo_at)
    qbd_at = place[0]
    qbd = sb("qbd", [P, NT, NB, P])
    work_at = place[0]
    ctxT = sb("ctxT", [P, 2, KD, SLP], F32R)
    probs = sb("probs", [P, SL])
    probsT = sb("probsT", [P, 2, NJ, P], F32R)
    qp = sb("qp", [P, 2, KD, P], F32R)
    o_lo = sb("o_lo", [P, D])
    o_sb = sb("o_sb", [P, D])
    oT = sb("oT", [P, KD, P])
    raw_at = place[0]
    raw = sb("raw", [P, NJ, D])
    ctxs_at = place[0]
    ctxs = sb("ctxs", [P, 2, NJ, 2, D], F32R)
    assert place[0] <= nc.sbuf_usable_end, place[0]

    nat = [sb(f"nat{n}", [P, NT, D] if n < 3 else [P, KD, HD], at=raw_at + n * 4 * HD * KD) for n in range(4)]
    assert raw_at + 4 * 4 * HD * KD <= ctxs_at + 4 * NJ * 2 * D
    wT = [sb(f"wT{n}", [P, KD, HD] if n < 3 else [P, NT, D], at=qbd_at + n * 4 * HD * KD) for n in range(4)]
    FB = 4 * NM * D
    fint = [sb(f"fint{n}", [P, NM, D] if n < 2 else [P, KD, HID], I32, at=raw_at + n * FB) for n in range(3)]
    fnat = [f[:].bitcast(F32) for f in fint]
    fT = [sb(f"fT{n}", [P, KD, HID] if n < 2 else [P, NM, D], at=raw_at + (3 + n) * FB) for n in range(3)]
    q2 = sb("q2", [P, NT, NB, P], at=work_at)
    kT2 = sb("kT2", [P, NT, TOK], at=work_at + 4 * NT * NB * P)
    assert work_at + 4 * NT * (NB * P + TOK) <= raw_at
    s1_at = ctxs_at + 4 * NJ * 2 * D
    v2 = sb("v2", [P, NI, HD], at=s1_at)
    att = sb("att", [P, 2, 2 * NT, SQ], at=s1_at + 4 * NI * HD)
    assert s1_at + 4 * (NI * HD + 4 * NT * SQ) <= place[0]
    hT = sb("hT", [P, NM, TOK], at=qbd_at)
    gs = sb("gs", [P, 2, TOK], at=qbd_at + 4 * NM * TOK)
    sg = sb("sg", [P, 2, TOK], at=qbd_at + 4 * (NM + 2) * TOK)

    x_tok = x.rearrange("b q d -> (b q) d").rearrange("(i p) d -> p i d", p=P)
    out_tok = out.rearrange("b q d -> (b q) d").rearrange("(i p) d -> p i d", p=P)

    def row(v, n):
        return v.rearrange("(a n) -> a n", a=1).broadcast_to([P, n])

    with ExitStack() as es:
        ps = es.enter_context(nc.psum_tensor("ps", [P, 8, 512], F32))
        SC, TP, ACC, MISC = 0, 4, 6, 7
        QB = [SC, SC + 1, SC + 2, SC + 3, SC, SC + 1, ACC, TP + 1]
        XT = [TP, TP, SC]

        def sem(name):
            return es.enter_context(nc.semaphore(name))

        x_loaded, wq_loaded, wk_loaded, wv_loaded = [sem(f"x_loaded{i}") for i in range(NI)], sem("wq_loaded"), sem("wk_loaded"), sem("wv_loaded")
        raw_loaded, rows_loaded, wo_loaded, nat_loaded, f_loaded = (
            sem("raw_loaded"), sem("rows_loaded"), sem("wo_loaded"), sem("nat_loaded"), sem("f_loaded"))
        ident_zeroed, ident_ready, pads_zeroed, qbd_zeroed, q2_zeroed = (
            sem("ident_zeroed"), sem("ident_ready"), sem("pads_zeroed"), sem("qbd_zeroed"), sem("q2_zeroed"))
        ln_stats, ln_mv, ln_veps, ln_std, ln_rstd, ln_done = (
            sem("ln_stats"), sem("ln_mv"), sem("ln_veps"), sem("ln_std"), sem("ln_rstd"), sem("ln_done"))
        xnT_filled, xnT_lo_copied, xnT_hi_copied = sem("xnT_filled"), sem("xnT_lo_copied"), sem("xnT_hi_copied")
        wkT_filled, wkT_copied, q_filled, q_low, q_high = (
            sem("wkT_filled"), sem("wkT_copied"), sem("q_filled"), sem("q_low"), sem("q_high"))
        ring_filled, ring_hi, ring_freed = sem("ring_filled"), sem("ring_hi"), sem("ring_freed")
        scores_filled, row_max, neg_max, exp_done, sum_done, rinv_ready = (
            sem("scores_filled"), sem("row_max"), sem("neg_max"), sem("exp_done"), sem("sum_done"), sem("rinv_ready"))
        av_filled, olo_ready, o_ready = sem("av_filled"), sem("olo_ready"), sem("o_ready")
        ot_filled, ot_copied, vp_filled, vp_low, vp_high = (
            sem("ot_filled"), sem("ot_copied"), sem("vp_filled"), sem("vp_low"), sem("vp_high"))
        qp_filled, qp_hi, qp_ready = sem("qp_filled"), sem("qp_hi"), sem("qp_ready")
        ctx_hi, ctx_lo, ctx_ready = sem("ctx_hi"), sem("ctx_lo"), sem("ctx_ready")
        wt_filled, wt_act, wt_dve, f_scaled = sem("wt_filled"), sem("wt_act"), sem("wt_dve"), sem("f_scaled")
        xb_ready, y_filled, x_ready = sem("xb_ready"), sem("y_filled"), sem("x_ready")
        p_filled, p_act, p_dve = sem("p_filled"), sem("p_act"), sem("p_dve")
        s_filled, col_max, s_shifted, s_exp, col_sum, col_inv, att_ready = (
            sem("s_filled"), sem("col_max"), sem("s_shifted"), sem("s_exp"), sem("col_sum"), sem("col_inv"), sem("att_ready"))
        c_filled, c_low, c_high = sem("c_filled"), sem("c_low"), sem("c_high")
        g_filled, g_sig, g_silu, h_ready = sem("g_filled"), sem("g_sig"), sem("g_silu"), sem("h_ready")
        stored = sem("stored")
        CORD = (1, 2, 3, 0)

        block = es.enter_context(nc.Block())

        def ct_base(b):
            return 0 if isinstance(b, int) and b == 0 else b * RING - NG

        def t_base(b, t, last):
            return NCT + b * RING + t * NG + (NCT if t > CT_STEP and not last else 0)

        def ring_bank(n):
            return TP + n % 2

        def wt_dest(n):
            if n < 16:
                w, c = wT[n // 4], n % 4
            else:
                w, c = fT[(n - 16) // 3], (n - 16) % 3
            return w[:].rearrange("p a b -> p (a b)")[:, c * 512:(c + 1) * 512]

        def wt_bank(n):
            return n % 8 if n < 16 else 4 + n % 4

        def batches(eng, step):
            for t in range(NT):
                step(0, t, True, False)
            with eng.Fori(1, NB - 1) as b:
                for t in range(NT):
                    step(b, t, False, False)
            for t in range(NT):
                step(NB - 1, t, False, True)

        @block.sync
        def _(sp):
            def load_raw(b):
                sp.dma_start(raw[:, 0:JF, :], ctx[b, 0:JF * P, :].rearrange("(p j) d -> p j d", j=JF)
                             ).then_inc(raw_loaded, 16)
                sp.dma_start(raw[0:JR, JF, :], ctx[b, JF * P:SL, :]).then_inc(raw_loaded, 16)

            for i in range(NI):
                sp.dma_start(xs[:, i, :], x_tok[:, i, :]).then_inc(x_loaded[i], 16)
            sp.dma_start(WQs[:], WQ.rearrange("(k p) n -> p k n", p=P)).then_inc(wq_loaded, 16)
            load_raw(0)
            sp.dma_start(WVs[:], WV.rearrange("(k p) n -> p k n", p=P)).then_inc(wv_loaded, 16)
            sp.wait_ge(ring_filled, NCT)
            sp.wait_ge(ctx_ready, 1)
            load_raw(1)
            with sp.Fori(2, NB) as b:
                sp.wait_ge(ring_filled, ct_base(b - 1) + NCT)
                sp.wait_ge(ctx_ready, b)
                load_raw(b)
            sp.wait_ge(ring_filled, ct_base(NB - 1) + NCT)
            sp.wait_ge(ctx_ready, NB)
            sp.wait_ge(av_filled, NT * (NB - 1))
            for n, w in enumerate((q_w, k_w, v_w)):
                sp.dma_start(nat[n][:], w.rearrange("h p d -> (h p) d").rearrange("(r p) d -> p r d", p=P)
                             ).then_inc(nat_loaded, 16)
            sp.dma_start(nat[3][:], l_w.rearrange("(k p) n -> p k n", p=P)).then_inc(nat_loaded, 16)
            sp.wait_ge(qp_filled, G)
            sp.dma_start(WOs[:], WO.rearrange("(t p) n -> p t n", p=P)).then_inc(wo_loaded, 16)
            sp.wait_ge(wt_filled, 16)
            for n, w in enumerate((w_gate, w_up, w_down)):
                sp.dma_start(fint[n][:], w.rearrange("(r p) d -> p r d", p=P)).then_inc(f_loaded, 16)
            for i in range(NI):
                sp.wait_ge(x_ready, 2 * NI + i + 1)
                sp.dma_start(out_tok[:, i, :], xs[:, i, :]).then_inc(stored, 16)
            sp.wait_ge(stored, 16 * NI)

        @block.gpsimd
        def _(pool):
            pool.memset(ident[:], 0.0).then_inc(ident_zeroed, 1)
            pool.wait_ge(ident_zeroed, 1)
            pool.affine_select(out=ident[:], in_=ident[:], compare_op=ALU.not_equal, fill=1.0, base=0,
                               pattern=[[-1, P]], channel_multiplier=1).then_inc(ident_ready, 1)
            pool.memset(ctxT[:, :, :, SL:SLP].bitcast(F32), 0.0).then_inc(pads_zeroed, 1)
            for half in range(2):
                lo, hi = half * DH, half * DH + DH
                if half:
                    pool.wait_ge(qbd_zeroed, 1)
                else:
                    pool.wait_ge(pads_zeroed, 1)
                pool.memset(qbd[lo:hi, :, :, DH - lo:P - lo], 0.0).then_inc(qbd_zeroed, 1)

            def split(b):
                pool.wait_ge(raw_loaded, 32 * b + 32)
                if isinstance(b, int) and b == 0:
                    pool.wait_ge(qbd_zeroed, 2)
                else:
                    pool.wait_ge(ctx_ready, b)
                parts = ((0, JF, P), (JF, NJ, JR))
                for n, (j0, j1, rows) in enumerate(parts):
                    if n:
                        pool.wait_ge(ctx_hi, 2 * b + 1)
                    pool.tensor_copy(ctxs[0:rows, b % 2, j0:j1, 0, :], raw[0:rows, j0:j1, :]).then_inc(ctx_hi, 1)
                pool.wait_ge(ctx_hi, 2 * b + 2)
                for n, (j0, j1, rows) in enumerate(parts):
                    if n:
                        pool.wait_ge(ctx_lo, b + 1)
                    pool.tensor_tensor(ctxs[0:rows, b % 2, j0:j1, 1, :], raw[0:rows, j0:j1, :],
                                       ctxs[0:rows, b % 2, j0:j1, 0, :].bitcast(F32), ALU.subtract
                                       ).then_inc(ctx_ready if n else ctx_lo, 1)

            split(0)
            split(1)
            with pool.Fori(2, NB) as b:
                pool.wait_ge(av_filled, NT * (b - 1))
                split(b)
            pool.wait_ge(vp_low, G)
            pool.wait_ge(vp_high, G)
            for half in range(2):
                lo, hi = half * DH, half * DH + DH
                if half:
                    pool.wait_ge(q2_zeroed, 1)
                else:
                    pool.wait_ge(ctx_ready, NB)
                pool.memset(q2[lo:hi, :, :, DH - lo:P - lo], 0.0).then_inc(q2_zeroed, 1)
            pool.wait_ge(q2_zeroed, 2)
            pool.wait_ge(f_loaded, 48)
            for n in range(3):
                pool.tensor_scalar(fnat[n], fint[n][:], 1.0 / 127.0, None, ALU.mult).then_inc(f_scaled, 1)

        @block.scalar
        def _(act):
            act.dma_start(WKs[:], WK.rearrange("(k p) n -> p k n", p=P)).then_inc(wk_loaded, 16)
            act.dma_start(bo_row[:], row(bO, D)).then_inc(rows_loaded, 16)
            act.dma_start(lb_row[:], row(l_b.rearrange("a n -> (a n)"), D)).then_inc(rows_loaded, 16)
            act.dma_start(vb_row[:], row(v_b.rearrange("h a p -> (h a p)"), HD)).then_inc(rows_loaded, 16)
            with nc.allow_non_contiguous_dma("one column per tile of two heads"):
                act.dma_start(qb_col[:], q_b.rearrange("(t h) a p -> (h a p) t", h=2)).then_inc(rows_loaded, 16)
                act.dma_start(kb_col[:], k_b.rearrange("(t h) a p -> (h a p) t", h=2)).then_inc(rows_loaded, 16)

            def table(func, n):
                act.wait_ge(ident_ready, 1)
                act.activation(warm[:, n:n + 1], ident[:, 0:1], func)

            def ln_sqrt(n, i):
                act.wait_ge(ln_veps, NI * n + i + 1)
                act.activation(std[:, i:i + 1], veps[:, i:i + 1], ACT.Sqrt).then_inc(ln_std, 1)

            def xnT_copy(n):
                act.wait_ge(xnT_filled, 2 * n + 1)
                act.activation(xnT[:, 0, :], ps[:, XT[n], :], ACT.Copy).then_inc(xnT_lo_copied, 1)

            table(ACT.Sqrt, 0)
            for i in range(NI):
                ln_sqrt(0, i)
            for c in range(4):
                act.wait_ge(wkT_filled, c + 1)
                act.activation(WKT[:, 2 * c:2 * c + 2, :].rearrange("p t d -> p (t d)"), ps[:, SC + c, :], ACT.Copy
                               ).then_inc(wkT_copied, 1)
            xnT_copy(0)
            def q_copy(t):
                act.wait_ge(q_filled, t + 1)
                act.activation(qbd[0:DH, t, :, 0:DH], ps[0:DH, QB[t], :].rearrange("p (b q) -> p b q", q=SQ),
                               ACT.Copy).then_inc(q_low, 1)

            def ct_hi(b, i):
                j0, j1 = CTG[i]
                w = (j1 - j0) * P if j1 < NJ else JR
                act.wait_ge(ring_filled, ct_base(b) + i + 1)
                src = ps[:, ring_bank(i), :].rearrange("p (k n) -> p k n", k=KD)[:, :, 0:w]
                act.activation(ctxT[:, 0, :, j0 * P:j0 * P + w], src, ACT.Copy).then_inc(ring_hi, 1)

            def t_hi(b, t, i, last):
                j0, j1 = GROUPS[i]
                rows = P if j1 < NJ else JR
                act.wait_ge(ring_filled, t_base(b, t, last) + i + 1)
                act.activation(probsT[0:rows, 0, j0:j1, :].rearrange("p j n -> p (j n)"),
                               ps[0:rows, ring_bank(i), 0:(j1 - j0) * P], ACT.Copy).then_inc(ring_hi, 1)

            def qp_split_hi(g):
                act.wait_ge(qp_filled, g + 1)
                act.activation(qp[:, 0, :, :].rearrange("p k n -> p (k n)"), ps[:, MISC, 0:D], ACT.Copy
                               ).then_inc(qp_hi, 1)

            def exps(g, par):
                act.wait_ge(neg_max, g + 1)
                act.activation(probs[:, 0:NC * CW].rearrange("p (c n) -> p c n", c=NC), ps[:, SC:SC + NC, 0:CW],
                               ACT.Exp, bias=negmax[:, par:par + 1], scale=SCALE, accum_out=expsum[:, par:par + 1])
                act.activation(probs[:, SL - 1:SL], ps[:, SC + NC - 1, CW:CW + 1], ACT.Exp,
                               bias=negmax[:, par:par + 1], scale=SCALE).then_inc(exp_done, 1)

            def o_scale_lo(g, par):
                act.wait_ge(av_filled, g + 1)
                act.wait_ge(rinv_ready, g + 1)
                act.wait_ge(o_ready, g)
                act.activation(o_lo[:], ps[:, ACC, D:2 * D], ACT.Copy, scale=rinv[:, par:par + 1]
                               ).then_inc(olo_ready, 1)

            def ot_copy(g):
                act.wait_ge(ot_filled, g + 1)
                act.activation(oT[:].rearrange("p k n -> p (k n)"), ps[:, MISC, 0:D], ACT.Copy).then_inc(ot_copied, 1)

            def heads_low(b, t, g):
                act.wait_ge(vp_filled, g + 1)
                act.activation(headsT[0:DH, t, bass.ds(b * SQ, SQ)], ps[0:DH, MISC, 0:DH], ACT.Copy).then_inc(vp_low, 1)

            act.wait_ge(qbd_zeroed, 2)
            q_copy(0)
            for i in range(NCT):
                if i % 2 == 0:
                    q_copy(i // 2 + 1)
                ct_hi(0, i)
            qp_split_hi(0)
            q_copy(5)
            table(ACT.Exp, 1)
            qp_split_hi(1)
            exps(0, 0)
            for t in range(6, NT):
                q_copy(t)

            def step(b, t, first, last):
                g = b * NT + t
                before = not (first and t == 0)
                pb, pt = (b, t - 1) if t else (b - 1, NT - 1)
                if before:
                    o_scale_lo(g - 1, (t + 1) % 2)
                t_hi(b, t, 0, last)
                t_hi(b, t, 1, last)
                if before:
                    ot_copy(g - 1)
                t_hi(b, t, 2, last)
                t_hi(b, t, 3, last)
                if before:
                    heads_low(pb, pt, g - 1)
                ct = t == CT_STEP and not last
                if not (last and t >= NT - 2):
                    qp_split_hi(g + 2)
                for i in range(2 if ct else 0):
                    ct_hi(b + 1, i)
                if not (last and t == NT - 1):
                    exps(g + 1, (t + 1) % 2)
                for i in range(2, NCT if ct else 0):
                    ct_hi(b + 1, i)

            batches(act, step)
            o_scale_lo(G - 1, (NT - 1) % 2)
            ot_copy(G - 1)
            heads_low(NB - 1, NT - 1, G - 1)

            def wt_copy(n, dst):
                act.wait_ge(wt_filled, n + 1)
                act.activation(dst, ps[:, wt_bank(n), :], ACT.Copy).then_inc(wt_act, 1)

            table(ACT.Sqrt, 2)
            for n in range(0, 16, 2):
                wt_copy(n, wt_dest(n))
            for i in range(NI):
                ln_sqrt(1, i)
            xnT_copy(1)
            table(ACT.Exp, 3)
            act.wait_ge(q2_zeroed, 2)
            for t in range(NT):
                act.wait_ge(p_filled, t + 1)
                act.activation(q2[0:DH, t, :, 0:DH], ps[0:DH, t % 4, :].rearrange("p (b q) -> p b q", q=SQ),
                               ACT.Identity, bias=qb_col[0:DH, t:t + 1]).then_inc(p_act, 1)
            for t in range(NT):
                act.wait_ge(p_filled, NT + t + 1)
                act.activation(kT2[:, t, :], ps[:, t % 4, :], ACT.Identity, bias=kb_col[:, t:t + 1]
                               ).then_inc(p_act, 1)

            def heads2_low(i):
                for n, c in enumerate(CORD):
                    act.wait_ge(c_filled, 4 * i + n + 1)
                    b = 2 * i + c // 2
                    t0 = (c % 2) * 4
                    act.activation(headsT[0:DH, t0:t0 + 4, b * SQ:(b + 1) * SQ],
                                   ps[0:DH, 4 + c, :].rearrange("p (t n) -> p t n", n=P)[:, :, 0:DH],
                                   ACT.Copy).then_inc(c_low, 1)

            def soft_exp(i):
                act.wait_ge(s_shifted, i + 1)
                act.activation(att[:, i % 2, :, :], att[:, i % 2, :, :], ACT.Exp, scale=SCALE).then_inc(s_exp, 1)

            for n in range(16, 18):
                wt_copy(n, wt_dest(n))
            soft_exp(0)
            for n in range(18, 22):
                wt_copy(n, wt_dest(n))
            soft_exp(1)
            for n in range(22, 25):
                wt_copy(n, wt_dest(n))
            for i in range(NI):
                heads2_low(i)
                if i + 2 < NI:
                    soft_exp(i + 2)
                if i == 1:
                    table(ACT.Sqrt, 4)
                if i == 2:
                    ln_sqrt(2, 0)
                    ln_sqrt(2, 1)
            ln_sqrt(2, 2)
            ln_sqrt(2, 3)
            table(ACT.Sigmoid, 5)
            xnT_copy(2)
            for m in range(NM):
                act.wait_ge(g_filled, 2 * m + 1)
                if m >= 2:
                    act.wait_ge(g_silu, m - 1)
                act.activation(sg[:, m % 2, :], ps[:, 2 * (m % 2), :], ACT.Sigmoid).then_inc(g_sig, 1)

        @block.vector
        def _(dve):
            def layer_norm(n, i, loads, value):
                m = NI * n + i + 1
                dve.wait_ge(loads, value)
                dve.bn_stats(stats[:, i, :], xs[:, i, :]).then_inc(ln_stats, 1)
                dve.wait_ge(ln_stats, m)
                dve.bn_aggr(meanvar[:, i, :], stats[:, i, :]).then_inc(ln_mv, 1)
                dve.wait_ge(ln_mv, m)
                dve.tensor_scalar(veps[:, i:i + 1], meanvar[:, i, 1:2], EPS, None, ALU.add).then_inc(ln_veps, 1)
                dve.wait_ge(ln_std, m)
                dve.reciprocal(rstd[:, i:i + 1], std[:, i:i + 1]).then_inc(ln_rstd, 1)
                dve.wait_ge(ln_rstd, m)
                dve.tensor_scalar(xn[:, i, :], xs[:, i, :], meanvar[:, i, 0:1], rstd[:, i:i + 1],
                                  ALU.subtract, ALU.mult).then_inc(ln_done, 1)

            def xnT_copy(n):
                dve.wait_ge(xnT_filled, 2 * n + 2)
                dve.tensor_copy(xnT[:, 1, :], ps[:, XT[n] + 1, :]).then_inc(xnT_hi_copied, 1)

            for i in range(NI):
                layer_norm(0, i, x_loaded[i], 16)
            xnT_copy(0)

            def q_copy(t):
                dve.wait_ge(q_filled, t + 1)
                dve.tensor_copy(qbd[DH:P, t, :, DH:P], ps[DH:P, QB[t], :].rearrange("p (b q) -> p b q", q=SQ)
                                ).then_inc(q_high, 1)

            def ct_lo(b, i):
                j0, j1 = CTG[i]
                w = (j1 - j0) * P if j1 < NJ else JR
                dve.wait_ge(ring_hi, ct_base(b) + i + 1)
                src = ps[:, ring_bank(i), :].rearrange("p (k n) -> p k n", k=KD)[:, :, 0:w]
                dve.tensor_tensor(ctxT[:, 1, :, j0 * P:j0 * P + w], src,
                                  ctxT[:, 0, :, j0 * P:j0 * P + w].bitcast(F32), ALU.subtract).then_inc(ring_freed, 1)

            def t_lo(b, t, i, last):
                j0, j1 = GROUPS[i]
                rows = P if j1 < NJ else JR
                dve.wait_ge(ring_hi, t_base(b, t, last) + i + 1)
                dve.tensor_tensor(probsT[0:rows, 1, j0:j1, :].rearrange("p j n -> p (j n)"),
                                  ps[0:rows, ring_bank(i), 0:(j1 - j0) * P],
                                  probsT[0:rows, 0, j0:j1, :].rearrange("p j n -> p (j n)").bitcast(F32),
                                  ALU.subtract).then_inc(ring_freed, 1)

            def qp_split_lo(g):
                dve.wait_ge(qp_hi, g + 1)
                dve.tensor_tensor(qp[:, 1, :, :].rearrange("p k n -> p (k n)"), ps[:, MISC, 0:D],
                                  qp[:, 0, :, :].rearrange("p k n -> p (k n)").bitcast(F32), ALU.subtract
                                  ).then_inc(qp_ready, 1)

            def maxima(g, par):
                dve.wait_ge(scores_filled, g + 1)
                dve.tensor_reduce(rowmax[:, par:par + 1], ps[:, SC:SC + NC, 0:CW], AX.XY, ALU.max).then_inc(row_max, 1)
                dve.wait_ge(row_max, g + 1)
                dve.tensor_scalar(negmax[:, par:par + 1], rowmax[:, par:par + 1], ps[:, SC + NC - 1, CW:CW + 1],
                                  -SCALE, ALU.max, ALU.mult).then_inc(neg_max, 1)

            def sums(g, par):
                dve.wait_ge(exp_done, g + 1)
                dve.tensor_tensor(rowsum[:, par:par + 1], expsum[:, par:par + 1], probs[:, SL - 1:SL], ALU.add
                                  ).then_inc(sum_done, 1)
                dve.wait_ge(sum_done, g + 1)
                dve.reciprocal(rinv[:, par:par + 1], rowsum[:, par:par + 1]).then_inc(rinv_ready, 1)

            def o_finish(g, par):
                dve.wait_ge(rinv_ready, g + 1)
                dve.wait_ge(olo_ready, g + 1)
                dve.scalar_tensor_tensor(out=o_sb[:], in0=ps[:, ACC, 0:D], scalar=rinv[:, par:par + 1], in1=o_lo[:],
                                         op0=ALU.mult, op1=ALU.add).then_inc(o_ready, 1)

            def heads_high(b, t, g):
                dve.wait_ge(vp_filled, g + 1)
                dve.tensor_copy(headsT[DH:P, t, bass.ds(b * SQ, SQ)], ps[DH:P, MISC, DH:P]).then_inc(vp_high, 1)

            dve.wait_ge(qbd_zeroed, 2)
            q_copy(0)
            for i in range(NCT):
                if i % 2 == 0:
                    q_copy(i // 2 + 1)
                ct_lo(0, i)
            qp_split_lo(0)
            q_copy(5)
            maxima(0, 0)
            qp_split_lo(1)
            for t in range(6, NT):
                q_copy(t)
            sums(0, 0)

            def step(b, t, first, last):
                g = b * NT + t
                before = not (first and t == 0)
                pb, pt = (b, t - 1) if t else (b - 1, NT - 1)
                if before:
                    o_finish(g - 1, (t + 1) % 2)
                for i in range(NG):
                    t_lo(b, t, i, last)
                if before:
                    heads_high(pb, pt, g - 1)
                ct = t == CT_STEP and not last
                if not (last and t == NT - 1):
                    maxima(g + 1, (t + 1) % 2)
                if not (last and t >= NT - 2):
                    qp_split_lo(g + 2)
                for i in range(2 if ct else 0):
                    ct_lo(b + 1, i)
                if not (last and t == NT - 1):
                    sums(g + 1, (t + 1) % 2)
                for i in range(2, NCT if ct else 0):
                    ct_lo(b + 1, i)

            batches(dve, step)
            o_finish(G - 1, (NT - 1) % 2)
            heads_high(NB - 1, NT - 1, G - 1)

            def wt_copy(n, dst):
                dve.wait_ge(wt_filled, n + 1)
                dve.tensor_copy(dst, ps[:, wt_bank(n), :]).then_inc(wt_dve, 1)

            def add_bias(n, bias):
                dve.wait_ge(rows_loaded, 16 * 5)
                for i in range(NI):
                    dve.tensor_tensor(xs[:, i, :], xs[:, i, :], bias[:], ALU.add).then_inc(xb_ready, 1)
                dve.wait_ge(xb_ready, NI * (n + 1))

            def add_y(n, i, bank):
                dve.wait_ge(y_filled, NI * n + i + 1)
                dve.tensor_tensor(xs[:, i, :], ps[:, bank, 0:D], xs[:, i, :], ALU.add).then_inc(x_ready, 1)

            for n in range(1, 16, 2):
                wt_copy(n, wt_dest(n))
            add_bias(0, bo_row)
            for i in range(NI):
                add_y(0, i, i)
                layer_norm(1, i, x_ready, i + 1)
            xnT_copy(1)
            dve.wait_ge(q2_zeroed, 2)
            for t in range(NT):
                dve.wait_ge(p_filled, t + 1)
                dve.tensor_scalar(q2[DH:P, t, :, DH:P], ps[DH:P, t % 4, :].rearrange("p (b q) -> p b q", q=SQ),
                                  qb_col[DH:P, t:t + 1], None, ALU.add).then_inc(p_dve, 1)
            for n in range(2 * NI):
                i, c = n // 2, n % 2
                dve.wait_ge(p_filled, 2 * NT + n + 1)
                dve.tensor_tensor(v2[:, i, c * 512:(c + 1) * 512], ps[:, 4 + n % 4, :],
                                  vb_row[:, c * 512:(c + 1) * 512], ALU.add).then_inc(p_dve, 1)
            add_bias(1, lb_row)

            def soft_shift(i):
                bank = 2 * (i % 2)
                sc = ps[:, bank:bank + 2, :].rearrange("p c (h q) -> p (c h) q", q=SQ)
                dve.wait_ge(s_filled, i + 1)
                dve.tensor_reduce(colmax[:, i % 2, :], sc, AX.X, ALU.max).then_inc(col_max, 1)
                dve.wait_ge(col_max, i + 1)
                if i >= 2:
                    dve.wait_ge(c_filled, 4 * (i - 1))
                dve.tensor_tensor(att[:, i % 2, :, :], sc, colmax[:, i % 2, :].unsqueeze(2).broadcast_to([P, 2 * NT, SQ]),
                                  ALU.subtract).then_inc(s_shifted, 1)

            def soft_norm(i):
                dve.wait_ge(s_exp, i + 1)
                dve.tensor_reduce(colsum[:, i % 2, :], att[:, i % 2, :, :], AX.X, ALU.add).then_inc(col_sum, 1)
                dve.wait_ge(col_sum, i + 1)
                dve.reciprocal(colinv[:, i % 2, :], colsum[:, i % 2, :]).then_inc(col_inv, 1)
                dve.wait_ge(col_inv, i + 1)
                dve.tensor_tensor(att[:, i % 2, :, :], att[:, i % 2, :, :],
                                  colinv[:, i % 2, :].unsqueeze(2).broadcast_to([P, 2 * NT, SQ]), ALU.mult).then_inc(att_ready, 1)

            def heads2_high(i):
                for n, c in enumerate(CORD):
                    dve.wait_ge(c_filled, 4 * i + n + 1)
                    b = 2 * i + c // 2
                    t0 = (c % 2) * 4
                    dve.tensor_copy(headsT[DH:P, t0:t0 + 4, b * SQ:(b + 1) * SQ],
                                    ps[DH:P, 4 + c, :].rearrange("p (t n) -> p t n", n=P)[:, :, DH:P]
                                    ).then_inc(c_high, 1)

            soft_shift(0)
            soft_shift(1)
            soft_norm(0)
            for i in range(NI):
                if i + 1 < NI:
                    soft_norm(i + 1)
                heads2_high(i)
                if i + 2 < NI:
                    soft_shift(i + 2)
                if i == 2:
                    layer_norm(2, 0, x_ready, NI + 1)
                    layer_norm(2, 1, x_ready, NI + 2)
                add_y(1, i, 4)
                if i >= 2:
                    layer_norm(2, i, x_ready, NI + i + 1)
            xnT_copy(2)
            for m in range(NM):
                dve.wait_ge(g_sig, m + 1)
                dve.tensor_tensor(gs[:, m % 2, :], ps[:, 2 * (m % 2), :], sg[:, m % 2, :], ALU.mult
                                  ).then_inc(g_silu, 1)
                dve.wait_ge(g_silu, m + 1)
                dve.wait_ge(g_filled, 2 * m + 2)
                dve.tensor_tensor(hT[:, m, :], ps[:, 2 * (m % 2) + 1, :], gs[:, m % 2, :], ALU.mult
                                  ).then_inc(h_ready, 1)
            for i in range(NI):
                add_y(2, i, 4 + i)

        @block.tensor
        def _(pe):
            def transpose_xn(n, i):
                pe.wait_ge(ln_done, NI * n + i + 1)
                for k in range(KD):
                    ins = pe.transpose(ps[:, XT[n] + k, i * P:(i + 1) * P], xn[:, i, k * P:(k + 1) * P], ident[:])
                    if i == NI - 1:
                        ins.then_inc(xnT_filled, 1)

            pe.wait_ge(ident_ready, 1)
            pe.wait_ge(wk_loaded, 16)
            for t in range(NT):
                for k in range(KD):
                    c = (t % 2) * D + k * P
                    ins = pe.transpose(ps[:, SC + t // 2, c:c + P], WKs[:, k, t * P:(t + 1) * P], ident[:])
                if t % 2:
                    ins.then_inc(wkT_filled, 1)
            for i in range(NI):
                transpose_xn(0, i)
            pe.wait_ge(wq_loaded, 16)
            pe.wait_ge(xnT_lo_copied, 1)
            pe.wait_ge(xnT_hi_copied, 1)

            def project_q(t):
                if t < 4:
                    pe.wait_ge(wkT_copied, t + 1)
                elif t < 6:
                    pe.wait_ge(q_low, t - 3)
                    pe.wait_ge(q_high, t - 3)
                for k in range(KD):
                    ins = pe.matmul(ps[:, QB[t], :], WQs[:, k, t * P:(t + 1) * P], xnT[:, k, :],
                                    start=(k == 0), stop=(k == KD - 1))
                ins.then_inc(q_filled, 1)

            def ctx_transposes(b, i):
                j0, j1 = CTG[i]
                n = ct_base(b) + i
                if not (isinstance(b, int) and b == 0 and i < 2):
                    pe.wait_ge(ring_freed, n - 1)
                for k in range(KD):
                    for j in range(j0, j1):
                        r = P if j < JF else JR
                        c = k * 2 * P + (j - j0) * P
                        ins = pe.transpose(ps[:, ring_bank(i), c:c + r], raw[0:r, j, k * P:(k + 1) * P],
                                           ident[0:r, 0:r])
                ins.then_inc(ring_filled, 1)

            def probs_transposes(b, t, i, last):
                j0, j1 = GROUPS[i]
                pe.wait_ge(ring_freed, t_base(b, t, last) + i - 1)
                for j in range(j0, j1):
                    r = P if j < JF else JR
                    c = (j - j0) * P
                    ins = pe.transpose(ps[0:r, ring_bank(i), c:c + P], probs[:, j * P:j * P + r], ident[:])
                ins.then_inc(ring_filled, 1)

            def q_by_wk(b, t, g):
                for k in range(KD):
                    ins = pe.matmul(ps[:, MISC, k * P:(k + 1) * P], WKT[:, t, k * P:(k + 1) * P], qbd[:, t, b, :],
                                    start=True, stop=True)
                ins.then_inc(qp_filled, 1)

            def scores_part(part):
                order = [(k, a, c) for k in range(KD) for a, c in ((0, 0), (0, 1), (1, 0))]
                runs = [(r, n) for r in range(len(order)) for n in range(NC)]
                for r, n in runs[6 * part:6 * part + 6]:
                    k, a, c = order[r]
                    w = CW if n < NC - 1 else CW + 2
                    ins = pe.matmul(ps[:, SC + n, 0:w], qp[:, a, k, :], ctxT[:, c, k, n * CW:n * CW + w],
                                    start=(r == 0), stop=(r == len(order) - 1))
                if part == 3:
                    ins.then_inc(scores_filled, 1)

            def o_transposes(g):
                pe.wait_ge(o_ready, g + 1)
                for k in range(KD):
                    ins = pe.transpose(ps[:, MISC, k * P:(k + 1) * P], o_sb[:, k * P:(k + 1) * P], ident[:])
                ins.then_inc(ot_filled, 1)

            def by_wv(t, g):
                pe.wait_ge(ot_copied, g + 1)
                for k in range(KD):
                    ins = pe.matmul(ps[:, MISC, 0:P], WVs[:, k, t * P:(t + 1) * P], oT[:, k, :],
                                    start=(k == 0), stop=(k == KD - 1))
                ins.then_inc(vp_filled, 1)

            project_q(0)
            for i in range(NCT):
                if i % 2 == 0:
                    project_q(i // 2 + 1)
                    pe.wait_ge(raw_loaded, 32)
                ctx_transposes(0, i)
            pe.wait_ge(q_low, 1)
            pe.wait_ge(q_high, 1)
            q_by_wk(0, 0, 0)
            project_q(5)
            pe.wait_ge(q_low, 6)
            pe.wait_ge(q_high, 6)
            pe.wait_ge(pads_zeroed, 1)
            pe.wait_ge(ring_freed, NCT)
            pe.wait_ge(qp_ready, 1)
            for part in range(4):
                scores_part(part)
            q_by_wk(0, 1, 1)
            for t in range(6, NT):
                project_q(t)
            pe.wait_ge(q_low, NT)
            pe.wait_ge(q_high, NT)
            pe.wait_ge(wv_loaded, 16)

            def step(b, t, first, last):
                g = b * NT + t
                before = not (first and t == 0)
                after = not (last and t == NT - 1)
                ct = t == CT_STEP and not last
                pt = t - 1 if t else NT - 1
                pe.wait_ge(exp_done, g + 1)
                if after:
                    pe.wait_ge(qp_ready, g + 2)
                    if t == NT - 1:
                        pe.wait_ge(ring_freed, ct_base(b + 1) + NCT)
                for i in range(NG):
                    probs_transposes(b, t, i, last)
                    if i == 2 and before:
                        pe.wait_ge(qp_ready, g + 2 if after else g + 1)
                        o_transposes(g - 1)
                    if after:
                        scores_part(i)
                if before:
                    by_wv(pt, g - 1)
                if before:
                    pe.wait_ge(o_ready, g)
                pe.wait_ge(ctx_ready, b + 1)
                cti = 0
                for j in range(NJ):
                    if ct and (j < 2 or j >= 7):
                        if j == 0:
                            pe.wait_ge(raw_loaded, 32 * b + 64)
                        ctx_transposes(b + 1, cti)
                        cti += 1
                    r = P if j < JF else JR
                    for i, (j0, j1) in enumerate(GROUPS):
                        if j == j0:
                            pe.wait_ge(ring_freed, t_base(b, t, last) + i + 1)
                    pe.matmul(ps[:, ACC, :], probsT[0:r, 0, j, :],
                              ctxs[0:r, b % 2, j, :, :].rearrange("p a d -> p (a d)"), start=(j == 0), stop=False)
                    ins = pe.matmul(ps[:, ACC, 0:D], probsT[0:r, 1, j, :], ctxs[0:r, b % 2, j, 0, :],
                                    start=False, stop=(j == NJ - 1))
                    if j == 2 and not (last and t >= NT - 2):
                        nb, nt = (b, t + 2) if t < NT - 2 else (b + 1, t + 2 - NT)
                        if before:
                            pe.wait_ge(vp_low, g)
                            pe.wait_ge(vp_high, g)
                        else:
                            pe.wait_ge(qp_ready, g + 2)
                        q_by_wk(nb, nt, g + 2)
                ins.then_inc(av_filled, 1)
                assert cti == (NCT if ct else 0)

            batches(pe, step)
            pe.wait_ge(vp_low, G - 1)
            pe.wait_ge(vp_high, G - 1)
            o_transposes(G - 1)
            by_wv(NT - 1, G - 1)

            def weight_transposes(n, pieces):
                if 8 <= n < 16:
                    s = wt_dve if n % 2 else wt_act
                    pe.wait_ge(s, (n - 8) // 2 + 1)
                elif n >= 20:
                    pe.wait_ge(wt_act, 8 + n - 19)
                for c, piece in enumerate(pieces):
                    ins = pe.transpose(ps[:, wt_bank(n), c * P:(c + 1) * P], piece, ident[:])
                ins.then_inc(wt_filled, 1)

            pe.wait_ge(vp_low, G)
            pe.wait_ge(vp_high, G)
            pe.wait_ge(nat_loaded, 64)
            for n in range(16):
                w, c = n // 4, n % 4
                if w < 3:
                    pieces = [nat[w][:, r % NT, (r // NT) * P:(r // NT + 1) * P] for r in range(4 * c, 4 * c + 4)]
                else:
                    pieces = [nat[w][:, r % KD, (r // KD) * P:(r // KD + 1) * P] for r in range(4 * c, 4 * c + 4)]
                weight_transposes(n, pieces)

            def project(src, w, i, bank):
                for t in range(NT):
                    ins = pe.matmul(ps[:, bank, 0:D], src[:, t, i * P:(i + 1) * P], w[:, t, :],
                                    start=(t == 0), stop=(t == NT - 1))
                ins.then_inc(y_filled, 1)

            pe.wait_ge(wo_loaded, 16)
            pe.wait_ge(wt_act, 8)
            pe.wait_ge(wt_dve, 8)
            for i in range(NI):
                project(headsT, WOs, i, i)
                if i:
                    transpose_xn(1, i - 1)
            transpose_xn(1, NI - 1)
            pe.wait_ge(xnT_lo_copied, 2)
            pe.wait_ge(xnT_hi_copied, 2)
            for n in range(2 * NT):
                t = n % NT
                if 4 <= n < NT + 4:
                    pe.wait_ge(p_act, n - 3)
                    pe.wait_ge(p_dve, n - 3)
                elif n >= NT + 4:
                    pe.wait_ge(p_act, n - 3)
                for k in range(KD):
                    ins = pe.matmul(ps[:, n % 4, :], wT[n // NT][:, k, t * P:(t + 1) * P], xnT[:, k, :],
                                    start=(k == 0), stop=(k == KD - 1))
                ins.then_inc(p_filled, 1)
            for n in range(2 * NI):
                i, c = n // 2, n % 2
                if n >= 4:
                    pe.wait_ge(p_dve, NT + n - 3)
                for k in range(KD):
                    ins = pe.matmul(ps[:, 4 + n % 4, :], xnT[:, k, i * P:(i + 1) * P],
                                    wT[2][:, k, c * 512:(c + 1) * 512], start=(k == 0), stop=(k == KD - 1))
                ins.then_inc(p_filled, 1)
            pe.wait_ge(p_act, 2 * NT)

            def self_scores(i):
                if i >= 2:
                    pe.wait_ge(s_shifted, i - 1)
                for t in range(NT):
                    bank = 2 * (i % 2) + t // 4
                    for e in range(2):
                        lo = e * SQ
                        ins = pe.matmul(ps[lo:lo + SQ, bank, (t % 4) * P:(t % 4 + 1) * P],
                                        kT2[:, t, i * P + lo:i * P + lo + SQ], q2[:, t, 2 * i + e, :],
                                        start=True, stop=True)
                ins.then_inc(s_filled, 1)

            def self_heads(i):
                pe.wait_ge(att_ready, i + 1)
                for c in CORD:
                    e, t0 = c // 2, (c % 2) * 4
                    lo = e * SQ
                    if i and c == 0:
                        pe.wait_ge(x_ready, NI + i)
                    for t in range(t0, t0 + 4):
                        ins = pe.matmul(ps[:, 4 + c, (t - t0) * P:(t - t0 + 1) * P],
                                        v2[lo:lo + SQ, i, t * P:(t + 1) * P],
                                        att[lo:lo + SQ, i % 2, 2 * t:2 * t + 2, :].rearrange("p h q -> p (h q)"),
                                        start=True, stop=True)
                    ins.then_inc(c_filled, 1)

            pe.wait_ge(p_dve, NT + 2 * NI)
            self_scores(0)
            self_scores(1)
            pe.wait_ge(f_scaled, 3)
            for n in range(16, 25):
                w, c = (n - 16) // 3, (n - 16) % 3
                if w < 2:
                    pieces = [fnat[w][:, r % NM, (r // NM) * P:(r // NM + 1) * P] for r in range(4 * c, 4 * c + 4)]
                else:
                    pieces = [fnat[w][:, r % KD, (r // KD) * P:(r // KD + 1) * P] for r in range(4 * c, 4 * c + 4)]
                weight_transposes(n, pieces)
            pe.wait_ge(wt_act, 17)
            for i in range(NI):
                self_heads(i)
                if i + 2 < NI:
                    self_scores(i + 2)
                pe.wait_ge(c_low, 4 * (i + 1))
                pe.wait_ge(c_high, 4 * (i + 1))
                project(headsT, wT[3], i, 4)
            for i in range(NI):
                transpose_xn(2, i)
            pe.wait_ge(xnT_lo_copied, 3)
            pe.wait_ge(xnT_hi_copied, 3)

            def gate_up(m):
                if m >= 2:
                    pe.wait_ge(h_ready, m - 1)
                for u in range(2):
                    for k in range(KD):
                        ins = pe.matmul(ps[:, 2 * (m % 2) + u, :], fT[u][:, k, m * P:(m + 1) * P], xnT[:, k, :],
                                        start=(k == 0), stop=(k == KD - 1))
                    ins.then_inc(g_filled, 1)

            def down(m):
                pe.wait_ge(h_ready, m + 1)
                for i in range(NI):
                    ins = pe.matmul(ps[:, 4 + i, 0:D], hT[:, m, i * P:(i + 1) * P], fT[2][:, m, :],
                                    start=(m == 0), stop=(m == NM - 1))
                    if m == NM - 1:
                        ins.then_inc(y_filled, 1)

            gate_up(0)
            for m in range(NM):
                if m + 1 < NM:
                    gate_up(m + 1)
                down(m)


_INS = ['x', 'ctx_1024', 'L0_xattn_WQ', 'L0_xattn_WK', 'L0_xattn_WV', 'L0_xattn_WO', 'L0_xattn_bO',
        'L0_attn_q_w', 'L0_attn_q_b', 'L0_attn_k_w', 'L0_attn_k_b', 'L0_attn_v_w', 'L0_attn_v_b',
        'L0_attn_l_w', 'L0_attn_l_b', 'L0_ffn_w_gate', 'L0_ffn_w_up', 'L0_ffn_w_down']
_OUTS = [((8, 64, 256), 'float32')]


def kernel(**inputs):
    import numpy as _np
    import concourse.bacc as _bacc
    from concourse import mybir as _mybir
    from concourse.bass_utils import run_bass_kernel_spmd as _run

    nc = _bacc.Bacc("TRN2", target_bir_lowering=False, num_devices=1)
    arrays, args = {}, []
    for name in _INS:
        a = _np.ascontiguousarray(inputs[name])
        arrays[f"in_{name}_dram"] = a
        args.append(nc.dram_tensor(f"in_{name}_dram", a.shape, _mybir.dt.from_np(a.dtype), kind="ExternalInput").ap())
    for i, (shape, dtype) in enumerate(_OUTS):
        dt = _mybir.dt.from_np(_np.dtype(dtype))
        args.append(nc.dram_tensor(f"out_{i}_dram", shape, dt, kind="ExternalOutput").ap())
    perceiver_layer(nc, *args)
    r = _run(nc, [arrays], core_ids=[0])
    return r.results[0]["out_0_dram"]
```

```python
from contextlib import ExitStack

import concourse.bass as bass
from concourse import mybir

F32 = mybir.dt.float32
F32R = mybir.dt.float32r
I32 = mybir.dt.int32
ALU = mybir.AluOpType
ACT = mybir.ActivationFunctionType
AX = mybir.AxisListType

P = 128
EPS = 1e-5
SBUF_START = 16512


def perceiver_layer(nc, x, ctx, WQ, WK, WV, WO, bO, q_w, q_b, k_w, k_b, v_w, v_b, l_w, l_b,
                    w_gate, w_up, w_down, out):
    NB, SQ, D = x.shape
    SL = ctx.shape[1]
    HD = WQ.shape[1]
    KD = D // P
    NT = HD // P
    DH = P // 2
    TOK = NB * SQ
    NI = TOK // P
    HT = TOK // 2
    G = NB * NT
    JF = SL // P
    JR = SL - JF * P
    NJ = JF + 1
    NC = 4
    CW = (SL - 1) // NC
    CL = (NC - 1) * CW
    SLP = NC * CW + 2
    HID = w_gate.shape[0]
    NM = HID // P
    SCALE = float(DH) ** -0.5
    assert NC * CW + 1 == SL and CW % 2 == 0 and SQ == DH and 0 < JR < P and NT == 8

    GROUPS = [(0, 4), (4, 8), (8, 12), (12, NJ)]
    CTG = [(0, 2), (2, 4), (4, 6), (6, 8), (8, 10), (10, 11), (11, 12), (12, NJ)]
    NG, NCT = len(GROUPS), len(CTG)
    RING = NT * NG + NCT
    CT_STEP = NT - 2
    CT_AT = (0, 1, 5, 8, 11)
    CT_EARLY = len(CT_AT)
    CT_NEED = [next(i for i, c in enumerate(CTG) if c[1] * P >= min((n + 1) * CW + 2 * (n == NC - 1), JF * P + 1)) + 1
               for n in range(NC)]

    place = [SBUF_START]

    def sb(name, shape, dt=F32, at=None):
        n = 4
        for s in shape[1:]:
            n *= s
        n = (n + 31) // 32 * 32
        if at is None:
            at = place[0]
            place[0] += n
        return nc.alloc_sbuf_tensor_at(name, shape, dt, offset=at)

    ident = sb("ident", [P, P])
    xs = sb("xs", [P, NI, D])
    bo_row = sb("bo_row", [P, D])
    lb_row = sb("lb_row", [P, D])
    qb_col = sb("qb_col", [P, NT])
    kb_col = sb("kb_col", [P, NT])
    stats = sb("stats", [P, NI, 6])
    meanvar = sb("meanvar", [P, NI, 2])
    veps = sb("veps", [P, NI])
    std = sb("std", [P, NI])
    rstd = sb("rstd", [P, NI])
    rowmax = sb("rowmax", [P, 2, 2])
    negmax = sb("negmax", [P, 2])
    expsum = sb("expsum", [P, 2, 2])
    rowsum = sb("rowsum", [P, 2])
    rinv = sb("rinv", [P, 2])
    warm = sb("warm", [P, 8])
    colmax = sb("colmax", [P, 2, 2 * NT])
    colsum = sb("colsum", [P, 2, 2 * NT])
    colinv = sb("colinv", [P, 2, 2 * NT])
    xn_at = place[0]
    xn = sb("xn", [P, NI, D])
    xnT = sb("xnT", [P, 2, KD, TOK], F32R)
    heads_at = place[0]
    headsT = sb("headsT", [P, NT, TOK])
    WQs = sb("WQs", [P, KD, HD], at=heads_at)
    WKs = sb("WKs", [P, KD, HD], at=heads_at + 4 * KD * HD)
    WVs = sb("WVs", [P, KD, HD])
    WVs_end = place[0]
    wo_at = place[0]
    WKT = sb("WKT", [P, NT, D])
    WOs = sb("WOs", [P, NT, D], at=wo_at)
    qbd_at = place[0]
    qbd = sb("qbd", [P, NT, NB, P])
    work_at = place[0]
    ctxT = sb("ctxT", [P, 2, KD, SLP], F32R)
    probs = sb("probs", [P, 2, SL])
    probsT = sb("probsT", [P, 2, NJ, P], F32R)
    qp = sb("qp", [P, 2, KD, P], F32R)
    o_lo = sb("o_lo", [P, D])
    o_sb = sb("o_sb", [P, D])
    oT = sb("oT", [P, KD, P])
    raw_at = place[0]
    raw = sb("raw", [P, NJ, D])
    ctxs_at = place[0]
    ctxs = sb("ctxs", [P, 2, NJ, 2, D], F32R)
    assert place[0] <= nc.sbuf_usable_end, place[0]

    W4 = 4 * HD * KD
    F4 = 4 * NM * D
    s1_at = ctxs_at + 4 * NJ * 2 * D
    WQp = sb("WQp", [P, 2, KD, HD], F32R, at=s1_at)

    nat = [sb("nat0", [P, NT, D], at=xn_at), sb("nat1", [P, NT, D], at=raw_at), sb("nat2", [P, NT, D], at=raw_at + W4),
           sb("nat3", [P, KD, HD], at=wo_at)]
    WOp = sb("WOp", [P, 2, NT, D], F32R, at=raw_at + 2 * W4)
    wp = [sb(f"wp{n}", [P, 2, KD, HD] if n < 3 else [P, 2, NT, D], F32R,
             at=(qbd_at if n < 2 else work_at) + (n % 2) * 2 * W4) for n in range(4)]
    headsP = [sb("headsP0", [P, NT, TOK], F32R, at=work_at + 4 * W4),
              sb("headsP1", [P, NT, TOK], F32R, at=raw_at + 4 * W4)]
    fint = [sb(f"fint{n}", [P, NM, D] if n < 2 else [P, KD, HID], I32, at=heads_at + n * F4) for n in range(3)]
    fnat = [f[:].bitcast(F32) for f in fint]
    vb_row = sb("vb_row", [P, HD], at=heads_at + 3 * F4)
    fp = [sb("fp0", [P, 2, KD, HID], F32R, at=work_at + 4 * W4),
          sb("fp1", [P, 2, KD, HID], F32R, at=work_at + 4 * W4 + 2 * F4),
          sb("fp2", [P, 2, NM, D], F32R, at=work_at)]
    q2_at = (work_at + 4 * W4 + 4 * F4 + 31) // 32 * 32
    q2 = sb("q2", [P, NT, NB, P], at=q2_at)
    kT2 = sb("kT2", [P, NT, TOK], at=q2_at + 4 * W4)
    v2 = sb("v2", [P, NI, HD], at=q2_at + 6 * W4)
    att = sb("att", [P, 2, 2 * NT, SQ], at=wo_at)
    heads2 = sb("heads2", [P, 2, NT, TOK], F32R, at=qbd_at)
    hTp = sb("hTp", [P, 2, NM, TOK], F32R, at=q2_at)
    gate_at = q2_at + 8 * NM * TOK
    sg, gs, hf = (sb(name, [P, 2, HT], at=gate_at + 8 * n * HT) for n, name in enumerate(("sg", "gs", "hf")))
    assert WVs_end - heads_at >= 3 * F4 + 4 * HD and q2_at >= raw_at and q2_at + 8 * W4 <= s1_at + 4 * NJ * 2 * D
    assert raw_at + 4 * W4 <= s1_at and gate_at + 24 * HT <= q2_at + 8 * W4

    x_tok = x.rearrange("b q d -> (b q) d").rearrange("(i p) d -> p i d", p=P)
    out_tok = out.rearrange("b q d -> (b q) d").rearrange("(i p) d -> p i d", p=P)

    def row(v, n):
        return v.rearrange("(a n) -> a n", a=1).broadcast_to([P, n])

    with ExitStack() as es:
        ps = es.enter_context(nc.psum_tensor("ps", [P, 8, 512], F32))
        SC, TP, ACC, MISC = 0, 4, 6, 7
        QB = [SC, SC + 1, SC + 2, SC + 3, SC, SC + 1, ACC, TP + 1]
        XT = [TP, SC, SC]
        HEAD_BANKS = [(2, 3, 0, 1), (4, 5, 6, 7), (0, 1, 6, 7), (2, 3, 4, 5)]
        SELF_BANK = [4, 6, 0, 2]
        Y_BANK = [[0, 1, 2, 3], [4, 5, 6, 7], [4, 5, 6, 7]]

        def sem(name):
            return es.enter_context(nc.semaphore(name))

        x_loaded, wv_loaded = [sem(f"x_loaded{i}") for i in range(NI)], sem("wv_loaded")
        wq_loaded, wk_loaded = ([sem(f"{w}_loaded{c}") for c in range(4)] for w in ("wq", "wk"))
        raw_loaded, rows_loaded, wo_loaded, nat_loaded, f_loaded = (
            sem("raw_loaded"), sem("rows_loaded"), sem("wo_loaded"), sem("nat_loaded"), sem("f_loaded"))
        ident_zeroed, ident_ready, pads_zeroed, qbd_zeroed, q2_zeroed = (
            sem("ident_zeroed"), sem("ident_ready"), sem("pads_zeroed"), sem("qbd_zeroed"), sem("q2_zeroed"))
        ln_stats, ln_mv, ln_veps, ln_std, ln_rstd, ln_done = (
            sem("ln_stats"), sem("ln_mv"), sem("ln_veps"), sem("ln_std"), sem("ln_rstd"), sem("ln_done"))
        xnT_filled, xnT_hi, xnT_ready = sem("xnT_filled"), sem("xnT_hi"), sem("xnT_ready")
        wq_hi, wq_ready = sem("wq_hi"), sem("wq_ready")
        wkT_filled, wkT_copied, q_filled, q_low, q_high = (
            sem("wkT_filled"), sem("wkT_copied"), sem("q_filled"), sem("q_low"), sem("q_high"))
        ring_filled, ring_hi, ring_freed = sem("ring_filled"), sem("ring_hi"), sem("ring_freed")
        scores_filled, row_max, neg_max, exp_done, sum_done, rinv_ready = (
            sem("scores_filled"), sem("row_max"), sem("neg_max"), sem("exp_done"), sem("sum_done"), sem("rinv_ready"))
        av_filled, olo_ready, o_ready = sem("av_filled"), sem("olo_ready"), sem("o_ready")
        ot_filled, ot_copied, vp_filled, vp_low, vp_high = (
            sem("ot_filled"), sem("ot_copied"), sem("vp_filled"), sem("vp_low"), sem("vp_high"))
        qp_filled, qp_hi, qp_ready = sem("qp_filled"), sem("qp_hi"), sem("qp_ready")
        ctx_hi, ctx_lo, ctx_ready = sem("ctx_hi"), sem("ctx_lo"), sem("ctx_ready")
        wt_filled, wt_hi, wt_ready, f_scaled = sem("wt_filled"), sem("wt_hi"), sem("wt_ready"), sem("f_scaled")
        wo_hi, wo_ready, hp_hi, hp_ready, nat3_loaded, vb_loaded = (
            sem("wo_hi"), sem("wo_ready"), sem("hp_hi"), sem("hp_ready"), sem("nat3_loaded"), sem("vb_loaded"))
        xb_ready, y_filled, x_ready = sem("xb_ready"), sem("y_filled"), sem("x_ready")
        p_filled, p_act, p_dve = sem("p_filled"), sem("p_act"), sem("p_dve")
        s_filled, col_max, s_shifted, s_exp, col_sum, col_inv, att_ready = (
            sem("s_filled"), sem("col_max"), sem("s_shifted"), sem("s_exp"), sem("col_sum"), sem("col_inv"), sem("att_ready"))
        c_filled, c_hi, c_ready = sem("c_filled"), sem("c_hi"), sem("c_ready")
        g_filled, g_sig, g_silu, h_full, h_hi, h_ready = (
            sem("g_filled"), sem("g_sig"), sem("g_silu"), sem("h_full"), sem("h_hi"), sem("h_ready"))
        stored = sem("stored")
        WT_N = 16 + 9
        FFN_N = 2 * NM

        PROJ = [(kind, h, n) for h in range(2) for kind, count in (("v", 4), ("q", NT), ("k", NT)) for n in range(count)]

        def dve_done(u):
            return sum(kind in "vq" for kind, _, _ in PROJ[:u + 1])

        def act_done(u):
            return sum(kind in "qk" for kind, _, _ in PROJ[:u + 1])

        def proj_bank(u):
            return (u + 2) % 4

        def wt_after(u):
            kind, h, n = PROJ[u]
            if h == 0:
                return 12 + n // 2 if kind == "q" and n % 2 == 0 else None
            return 16 + n if kind == "q" else 16 + NT if kind == "k" and n == 0 else None

        def heads2_piece(i, c, half, part):
            b, t0, lo = 2 * i + c // 2, (c % 2) * 4, half * DH
            return (heads2[lo:lo + DH, part, t0:t0 + 4, b * SQ:(b + 1) * SQ],
                    ps[lo:lo + DH, HEAD_BANKS[i][c], :].rearrange("p (t n) -> p t n", n=P)[:, :, lo:lo + DH])

        def xnT_half(part, h):
            return xnT[:, part, :, h * HT:(h + 1) * HT]

        def xnT_bank(n, h):
            return ps[:, XT[n] + h, :].rearrange("p (k n) -> p k n", k=KD)

        block = es.enter_context(nc.Block())

        def ct_base(b):
            return 0 if isinstance(b, int) and b == 0 else b * RING - NG

        def t_base(b, t, last):
            return NCT + b * RING + t * NG + (NCT if t > CT_STEP and not last else 0)

        def ring_bank(n):
            return TP + n % 2

        def wt_dest(n, part):
            w, c = (wp[n // 4], n % 4) if n < 16 else (fp[(n - 16) // 3], (n - 16) % 3)
            return w[:, part, :, :].rearrange("p a b -> p (a b)")[:, c * 512:(c + 1) * 512]

        def wt_bank(n):
            return n if n < 4 else 4 + n % 4

        def batches(eng, step):
            for t in range(NT):
                step(0, t, True, False)
            with eng.Fori(1, NB - 1) as b:
                for t in range(NT):
                    step(b, t, False, False)
            for t in range(NT):
                step(NB - 1, t, False, True)

        @block.sync
        def _(sp):
            def load_raw(b):
                sp.dma_start(raw[:, 0:JF, :], ctx[b, 0:JF * P, :].rearrange("(p j) d -> p j d", j=JF)
                             ).then_inc(raw_loaded, 16)
                sp.dma_start(raw[0:JR, JF, :], ctx[b, JF * P:SL, :]).then_inc(raw_loaded, 16)

            for i in range(0, NI, 2):
                sp.dma_start(xs[:, i, :], x_tok[:, i, :]).then_inc(x_loaded[i], 16)
            for dst, w, loaded in ((WKs, WK, wk_loaded), (WQs, WQ, wq_loaded)):
                for c in range(4):
                    sp.dma_start(dst[:, :, c * D:(c + 1) * D], w.rearrange("(k p) n -> p k n", p=P)[:, :, c * D:(c + 1) * D]
                                 ).then_inc(loaded[c], 16)
            load_raw(0)
            sp.dma_start(WVs[:], WV.rearrange("(k p) n -> p k n", p=P)).then_inc(wv_loaded, 16)
            sp.wait_ge(ring_filled, NCT)
            sp.wait_ge(ctx_ready, 1)
            load_raw(1)
            with sp.Fori(2, NB) as b:
                sp.wait_ge(ring_filled, ct_base(b - 1) + NCT)
                sp.wait_ge(ctx_ready, b)
                load_raw(b)
            sp.wait_ge(ring_filled, ct_base(NB - 1) + NCT)
            sp.wait_ge(ctx_ready, NB)
            sp.wait_ge(av_filled, NT * (NB - 1))
            for n, w in enumerate((q_w, k_w, v_w)):
                sp.dma_start(nat[n][:], w.rearrange("h p d -> (h p) d").rearrange("(r p) d -> p r d", p=P)
                             ).then_inc(nat_loaded, 16)
            sp.wait_ge(qp_filled, G)
            sp.dma_start(WOs[:], WO.rearrange("(t p) n -> p t n", p=P)).then_inc(wo_loaded, 16)
            sp.wait_ge(vp_filled, G)
            sp.wait_ge(hp_ready, NI)
            sp.dma_start(vb_row[:], row(v_b.rearrange("h a p -> (h a p)"), HD)).then_inc(vb_loaded, 16)
            sp.wait_ge(wo_ready, 1)
            sp.dma_start(nat[3][:], l_w.rearrange("(k p) n -> p k n", p=P)).then_inc(nat3_loaded, 16)
            for n, w in enumerate((w_gate, w_up, w_down)):
                sp.dma_start(fint[n][:], w.rearrange("(r p) d -> p r d", p=P)).then_inc(f_loaded, 16)
            for i in range(NI):
                sp.wait_ge(x_ready, 2 * NI + i + 1)
                sp.dma_start(out_tok[:, i, :], xs[:, i, :]).then_inc(stored, 16)
            sp.wait_ge(stored, 16 * NI)

        @block.gpsimd
        def _(pool):
            pool.memset(ident[:], 0.0).then_inc(ident_zeroed, 1)
            pool.wait_ge(ident_zeroed, 1)
            pool.affine_select(out=ident[:], in_=ident[:], compare_op=ALU.not_equal, fill=1.0, base=0,
                               pattern=[[-1, P]], channel_multiplier=1).then_inc(ident_ready, 1)
            pool.memset(ctxT[:, :, :, SL:SLP].bitcast(F32), 0.0).then_inc(pads_zeroed, 1)
            for half in range(2):
                lo, hi = half * DH, half * DH + DH
                if half:
                    pool.wait_ge(qbd_zeroed, 1)
                else:
                    pool.wait_ge(pads_zeroed, 1)
                pool.memset(qbd[lo:hi, :, :, DH - lo:P - lo], 0.0).then_inc(qbd_zeroed, 1)

            def split(b):
                pool.wait_ge(raw_loaded, 32 * b + 32)
                if isinstance(b, int) and b == 0:
                    pool.wait_ge(qbd_zeroed, 2)
                else:
                    pool.wait_ge(ctx_ready, b)
                parts = ((0, JF, P), (JF, NJ, JR))
                for n, (j0, j1, rows) in enumerate(parts):
                    if n:
                        pool.wait_ge(ctx_hi, 2 * b + 1)
                    pool.tensor_copy(ctxs[0:rows, b % 2, j0:j1, 0, :], raw[0:rows, j0:j1, :]).then_inc(ctx_hi, 1)
                pool.wait_ge(ctx_hi, 2 * b + 2)
                for n, (j0, j1, rows) in enumerate(parts):
                    if n:
                        pool.wait_ge(ctx_lo, b + 1)
                    pool.tensor_tensor(ctxs[0:rows, b % 2, j0:j1, 1, :], raw[0:rows, j0:j1, :],
                                       ctxs[0:rows, b % 2, j0:j1, 0, :].bitcast(F32), ALU.subtract
                                       ).then_inc(ctx_ready if n else ctx_lo, 1)

            split(0)
            pool.wait_ge(q_filled, NT)
            split(1)
            with pool.Fori(2, NB) as b:
                pool.wait_ge(av_filled, NT * (b - 1))
                split(b)
            pool.wait_ge(wo_loaded, 16)
            pool.wait_ge(ring_filled, ct_base(NB - 1) + NCT)
            pool.wait_ge(av_filled, NT * (NB - 1))
            pool.tensor_copy(WOp[:, 0, :, :], WOs[:]).then_inc(wo_hi, 1)
            pool.wait_ge(wo_hi, 1)
            pool.tensor_tensor(WOp[:, 1, :, :], WOs[:], WOp[:, 0, :, :].bitcast(F32), ALU.subtract).then_inc(wo_ready, 1)
            for i in range(1, NI):
                pool.wait_ge(hp_hi, i + 1)
                if i == 1:
                    pool.wait_ge(hp_ready, 1)
                pool.tensor_tensor(headsP[1][:, :, i * P:(i + 1) * P], headsT[:, :, i * P:(i + 1) * P],
                                   headsP[0][:, :, i * P:(i + 1) * P].bitcast(F32), ALU.subtract).then_inc(hp_ready, 1)
            pool.wait_ge(y_filled, NI)
            for half in range(2):
                lo, hi = half * DH, half * DH + DH
                if half:
                    pool.wait_ge(q2_zeroed, 1)
                else:
                    pool.wait_ge(hp_ready, NI)
                pool.memset(q2[lo:hi, :, :, DH - lo:P - lo], 0.0).then_inc(q2_zeroed, 1)
            pool.wait_ge(q2_zeroed, 2)
            pool.wait_ge(f_loaded, 48)
            for n in range(3):
                pool.tensor_scalar(fnat[n], fint[n][:], 1.0 / 127.0, None, ALU.mult).then_inc(f_scaled, 1)

        @block.scalar
        def _(act):
            for i in range(1, NI, 2):
                act.dma_start(xs[:, i, :], x_tok[:, i, :]).then_inc(x_loaded[i], 16)
            def table(func, n):
                act.wait_ge(ident_ready, 1)
                act.activation(warm[:, n:n + 1], ident[:, 0:1], func)

            def ln_sqrt(n, i):
                act.wait_ge(ln_veps, NI * n + i + 1)
                act.activation(std[:, i:i + 1], veps[:, i:i + 1], ACT.Sqrt).then_inc(ln_std, 1)

            def xnT_split_hi(n, h):
                act.wait_ge(xnT_filled, 2 * n + h + 1)
                act.activation(xnT_half(0, h), xnT_bank(n, h), ACT.Copy).then_inc(xnT_hi, 1)

            def wkT_copy(c):
                act.wait_ge(wkT_filled, c + 1)
                act.activation(WKT[:, 2 * c:2 * c + 2, :].rearrange("p t d -> p (t d)"), ps[:, SC + c, :], ACT.Copy
                               ).then_inc(wkT_copied, 1)

            def wq_split_hi(c):
                act.wait_ge(wq_loaded[c], 16)
                act.activation(WQp[:, 0, :, c * D:(c + 1) * D], WQs[:, :, c * D:(c + 1) * D], ACT.Copy).then_inc(wq_hi, 1)

            table(ACT.Sqrt, 0)
            for i in range(NI):
                ln_sqrt(0, i)
            wkT_copy(0)
            wkT_copy(1)
            xnT_split_hi(0, 0)
            xnT_split_hi(0, 1)
            wq_split_hi(0)
            wkT_copy(2)
            wkT_copy(3)
            for c in range(1, 4):
                wq_split_hi(c)
            act.dma_start(bo_row[:], row(bO, D)).then_inc(rows_loaded, 16)
            act.dma_start(lb_row[:], row(l_b.rearrange("a n -> (a n)"), D)).then_inc(rows_loaded, 16)
            with nc.allow_non_contiguous_dma("one column per tile of two heads"):
                act.dma_start(qb_col[:], q_b.rearrange("(t h) a p -> (h a p) t", h=2)).then_inc(rows_loaded, 16)
                act.dma_start(kb_col[:], k_b.rearrange("(t h) a p -> (h a p) t", h=2)).then_inc(rows_loaded, 16)

            def q_copy(t):
                act.wait_ge(q_filled, t + 1)
                act.activation(qbd[0:DH, t, :, 0:DH], ps[0:DH, QB[t], :].rearrange("p (b q) -> p b q", q=SQ),
                               ACT.Copy).then_inc(q_low, 1)

            def ct_hi(b, i):
                j0, j1 = CTG[i]
                w = (j1 - j0) * P if j1 < NJ else JR
                act.wait_ge(ring_filled, ct_base(b) + i + 1)
                src = ps[:, ring_bank(i), :].rearrange("p (k n) -> p k n", k=KD)[:, :, 0:w]
                act.activation(ctxT[:, 0, :, j0 * P:j0 * P + w], src, ACT.Copy).then_inc(ring_hi, 1)

            def t_hi(b, t, i, last):
                j0, j1 = GROUPS[i]
                rows = P if j1 < NJ else JR
                act.wait_ge(ring_filled, t_base(b, t, last) + i + 1)
                act.activation(probsT[0:rows, 0, j0:j1, :].rearrange("p j n -> p (j n)"),
                               ps[0:rows, ring_bank(i), 0:(j1 - j0) * P], ACT.Copy).then_inc(ring_hi, 1)

            def qp_split_hi(g):
                act.wait_ge(qp_filled, g + 1)
                act.activation(qp[:, 0, :, :].rearrange("p k n -> p (k n)"), ps[:, MISC, 0:D], ACT.Copy
                               ).then_inc(qp_hi, 1)

            def exps(g, par):
                act.wait_ge(neg_max, g + 1)
                act.activation(probs[:, par, 0:CL].rearrange("p (c n) -> p c n", c=NC - 1), ps[:, SC:SC + NC - 1, 0:CW],
                               ACT.Exp, bias=negmax[:, par:par + 1], scale=SCALE, accum_out=expsum[:, par, 0:1])
                act.activation(probs[:, par, CL:SL], ps[:, SC + NC - 1, 0:SL - CL], ACT.Exp, bias=negmax[:, par:par + 1],
                               scale=SCALE, accum_out=expsum[:, par, 1:2]).then_inc(exp_done, 1)

            def o_scale_lo(g, par):
                act.wait_ge(av_filled, g + 1)
                act.wait_ge(rinv_ready, g + 1)
                act.wait_ge(o_ready, g)
                act.activation(o_lo[:], ps[:, ACC, D:2 * D], ACT.Copy, scale=rinv[:, par:par + 1]
                               ).then_inc(olo_ready, 1)

            def ot_copy(g):
                act.wait_ge(ot_filled, g + 1)
                act.activation(oT[:].rearrange("p k n -> p (k n)"), ps[:, MISC, 0:D], ACT.Copy).then_inc(ot_copied, 1)

            def heads_low(b, t, g):
                act.wait_ge(vp_filled, g + 1)
                act.activation(headsT[0:DH, t, bass.ds(b * SQ, SQ)], ps[0:DH, MISC, 0:DH], ACT.Copy).then_inc(vp_low, 1)

            act.wait_ge(qbd_zeroed, 2)
            for t in range(3):
                q_copy(t)
            for i in range(NCT):
                ct_hi(0, i)
                if i == 5:
                    qp_split_hi(0)
                if i % 2 and i < 6:
                    q_copy(i // 2 + 3)
            table(ACT.Exp, 1)
            qp_split_hi(1)
            exps(0, 0)
            for t in range(6, NT):
                q_copy(t)

            def step(b, t, first, last):
                g = b * NT + t
                before = not (first and t == 0)
                pb, pt = (b, t - 1) if t else (b - 1, NT - 1)
                ct = t == CT_STEP and not last
                spread = t == NT - 1 and not last
                if before:
                    o_scale_lo(g - 1, (t + 1) % 2)
                if spread:
                    for i in range(CT_EARLY, NCT):
                        ct_hi(b + 1, i)
                    ot_copy(g - 1)
                    t_hi(b, t, 0, last)
                    t_hi(b, t, 1, last)
                else:
                    t_hi(b, t, 0, last)
                    t_hi(b, t, 1, last)
                    if before:
                        ot_copy(g - 1)
                    t_hi(b, t, 2, last)
                    t_hi(b, t, 3, last)
                if before:
                    heads_low(pb, pt, g - 1)
                if spread:
                    t_hi(b, t, 2, last)
                for i in range(2 if ct else 0):
                    ct_hi(b + 1, i)
                if not (last and t == NT - 1):
                    exps(g + 1, (t + 1) % 2)
                if not (last and t >= NT - 2):
                    qp_split_hi(g + 2)
                for i in range(2, CT_EARLY if ct else 0):
                    ct_hi(b + 1, i)
                if spread:
                    t_hi(b, t, 3, last)

            batches(act, step)
            def wt_split_hi(n):
                act.wait_ge(wt_filled, n + 1)
                act.activation(wt_dest(n, 0), ps[:, wt_bank(n), :], ACT.Copy).then_inc(wt_hi, 1)

            def heads_split_hi(i):
                act.wait_ge(vp_low, 2 * NT * (i + 1))
                act.wait_ge(vp_high, 2 * NT * (i + 1))
                act.activation(headsP[0][:, :, i * P:(i + 1) * P], headsT[:, :, i * P:(i + 1) * P], ACT.Copy
                               ).then_inc(hp_hi, 1)

            def wts(*ns):
                for n in ns:
                    wt_split_hi(n)

            o_scale_lo(G - 1, (NT - 1) % 2)
            heads_split_hi(0)
            ot_copy(G - 1)
            wts(0)
            heads_split_hi(1)
            wts(1)
            heads_low(NB - 1, NT - 1, G - 1)
            wts(2, 3, 4)
            table(ACT.Sqrt, 2)
            wts(5, 6)
            heads_split_hi(2)
            ln_sqrt(1, 0)
            heads_split_hi(3)
            wts(7)
            ln_sqrt(1, 1)
            wts(8, 9)
            xnT_split_hi(1, 0)
            wts(10)
            ln_sqrt(1, 2)
            wts(11)
            ln_sqrt(1, 3)
            xnT_split_hi(1, 1)
            table(ACT.Exp, 3)

            def soft_exp(i):
                act.wait_ge(s_shifted, i + 1)
                act.activation(att[:, i % 2, :, :], att[:, i % 2, :, :], ACT.Exp, scale=SCALE).then_inc(s_exp, 1)

            act.wait_ge(q2_zeroed, 2)
            for u, (kind, h, t) in enumerate(PROJ):
                if kind == "v" and h == 1 and t == 0:
                    soft_exp(0)
                    soft_exp(1)
                if kind != "v":
                    act.wait_ge(p_filled, u + 1)
                if kind == "q":
                    act.activation(q2[0:DH, t, 4 * h:4 * h + 4, 0:DH],
                                   ps[0:DH, proj_bank(u), 0:HT].rearrange("p (b q) -> p b q", q=SQ),
                                   ACT.Identity, bias=qb_col[0:DH, t:t + 1]).then_inc(p_act, 1)
                if kind == "k":
                    act.activation(kT2[:, t, h * HT:(h + 1) * HT], ps[:, proj_bank(u), 0:HT], ACT.Identity,
                                   bias=kb_col[:, t:t + 1]).then_inc(p_act, 1)
                if wt_after(u) is not None:
                    wt_split_hi(wt_after(u))

            def heads2_hi(i):
                for c in range(4):
                    act.wait_ge(c_filled, 4 * i + c + 1)
                    for half in range(2):
                        dst, src = heads2_piece(i, c, half, 0)
                        ins = act.activation(dst, src, ACT.Copy)
                    ins.then_inc(c_hi, 1)

            heads2_hi(0)
            heads2_hi(1)
            soft_exp(2)
            soft_exp(3)
            table(ACT.Sqrt, 4)
            heads2_hi(2)
            ln_sqrt(2, 0)
            ln_sqrt(2, 1)
            heads2_hi(3)
            xnT_split_hi(2, 0)
            ln_sqrt(2, 2)
            ln_sqrt(2, 3)
            table(ACT.Sigmoid, 5)

            def sigmoids(u):
                act.wait_ge(g_filled, u + 1)
                if u >= 2:
                    act.wait_ge(g_silu, u - 1)
                act.activation(sg[:, u % 2, :], ps[:, proj_bank(u), 0:HT], ACT.Sigmoid).then_inc(g_sig, 1)

            def h_split_hi(u):
                act.wait_ge(h_full, u + 1)
                act.activation(hTp[:, 0, u % NM, (u // NM) * HT:(u // NM + 1) * HT], hf[:, u % 2, :], ACT.Copy
                               ).then_inc(h_hi, 1)

            sigmoids(0)
            xnT_split_hi(2, 1)
            for u in range(FFN_N):
                if u + 1 < FFN_N:
                    sigmoids(u + 1)
                h_split_hi(u)

        @block.vector
        def _(dve):
            def ln_first(n, i):
                m = NI * n + i + 1
                dve.wait_ge(x_ready, NI * (n - 1) + i + 1)
                dve.bn_stats(stats[:, i, :], xs[:, i, :]).then_inc(ln_stats, 1)
                dve.wait_ge(ln_stats, m)
                dve.bn_aggr(meanvar[:, i, :], stats[:, i, :]).then_inc(ln_mv, 1)
                dve.wait_ge(ln_mv, m)
                dve.tensor_scalar(veps[:, i:i + 1], meanvar[:, i, 1:2], EPS, None, ALU.add).then_inc(ln_veps, 1)

            def ln_last(n, i):
                m = NI * n + i + 1
                dve.wait_ge(ln_std, m)
                dve.reciprocal(rstd[:, i:i + 1], std[:, i:i + 1]).then_inc(ln_rstd, 1)
                dve.wait_ge(ln_rstd, m)
                dve.tensor_scalar(xn[:, i, :], xs[:, i, :], meanvar[:, i, 0:1], rstd[:, i:i + 1],
                                  ALU.subtract, ALU.mult).then_inc(ln_done, 1)

            def xnT_split_lo(n, h):
                dve.wait_ge(xnT_hi, 2 * n + h + 1)
                dve.tensor_tensor(xnT_half(1, h), xnT_bank(n, h), xnT_half(0, h).bitcast(F32),
                                  ALU.subtract).then_inc(xnT_ready, 1)

            for i in range(NI):
                dve.wait_ge(x_loaded[i], 16)
                dve.bn_stats(stats[:, i, :], xs[:, i, :]).then_inc(ln_stats, 1)
            for i in range(NI):
                dve.wait_ge(ln_stats, i + 1)
                dve.bn_aggr(meanvar[:, i, :], stats[:, i, :]).then_inc(ln_mv, 1)
            for i in range(NI):
                dve.wait_ge(ln_mv, i + 1)
                dve.tensor_scalar(veps[:, i:i + 1], meanvar[:, i, 1:2], EPS, None, ALU.add).then_inc(ln_veps, 1)
            for i in range(NI):
                dve.wait_ge(ln_std, i + 1)
                dve.reciprocal(rstd[:, i:i + 1], std[:, i:i + 1]).then_inc(ln_rstd, 1)
            for i in range(NI):
                dve.wait_ge(ln_rstd, i + 1)
                dve.tensor_scalar(xn[:, i, :], xs[:, i, :], meanvar[:, i, 0:1], rstd[:, i:i + 1],
                                  ALU.subtract, ALU.mult).then_inc(ln_done, 1)
            xnT_split_lo(0, 0)
            xnT_split_lo(0, 1)
            for c in range(4):
                dve.wait_ge(wq_hi, c + 1)
                dve.tensor_tensor(WQp[:, 1, :, c * D:(c + 1) * D], WQs[:, :, c * D:(c + 1) * D],
                                  WQp[:, 0, :, c * D:(c + 1) * D].bitcast(F32), ALU.subtract).then_inc(wq_ready, 1)

            def q_copy(t):
                dve.wait_ge(q_filled, t + 1)
                dve.tensor_copy(qbd[DH:P, t, :, DH:P], ps[DH:P, QB[t], :].rearrange("p (b q) -> p b q", q=SQ)
                                ).then_inc(q_high, 1)

            def ct_lo(b, i):
                j0, j1 = CTG[i]
                w = (j1 - j0) * P if j1 < NJ else JR
                dve.wait_ge(ring_hi, ct_base(b) + i + 1)
                src = ps[:, ring_bank(i), :].rearrange("p (k n) -> p k n", k=KD)[:, :, 0:w]
                dve.tensor_tensor(ctxT[:, 1, :, j0 * P:j0 * P + w], src,
                                  ctxT[:, 0, :, j0 * P:j0 * P + w].bitcast(F32), ALU.subtract).then_inc(ring_freed, 1)

            def t_lo(b, t, i, last):
                j0, j1 = GROUPS[i]
                rows = P if j1 < NJ else JR
                dve.wait_ge(ring_hi, t_base(b, t, last) + i + 1)
                dve.tensor_tensor(probsT[0:rows, 1, j0:j1, :].rearrange("p j n -> p (j n)"),
                                  ps[0:rows, ring_bank(i), 0:(j1 - j0) * P],
                                  probsT[0:rows, 0, j0:j1, :].rearrange("p j n -> p (j n)").bitcast(F32),
                                  ALU.subtract).then_inc(ring_freed, 1)

            def qp_split_lo(g):
                dve.wait_ge(qp_hi, g + 1)
                dve.tensor_tensor(qp[:, 1, :, :].rearrange("p k n -> p (k n)"), ps[:, MISC, 0:D],
                                  qp[:, 0, :, :].rearrange("p k n -> p (k n)").bitcast(F32), ALU.subtract
                                  ).then_inc(qp_ready, 1)

            def max_first(g, par):
                dve.wait_ge(scores_filled, 2 * g + 1)
                dve.tensor_reduce(rowmax[:, par, 0:1], ps[:, SC:SC + NC - 1, 0:CW], AX.XY, ALU.max)

            def max_last(g, par):
                dve.wait_ge(scores_filled, 2 * g + 2)
                dve.tensor_reduce(rowmax[:, par, 1:2], ps[:, SC + NC - 1, 0:SL - CL], AX.X, ALU.max).then_inc(row_max, 1)
                dve.wait_ge(row_max, g + 1)
                dve.tensor_scalar(negmax[:, par:par + 1], rowmax[:, par, 0:1], rowmax[:, par, 1:2],
                                  -SCALE, ALU.max, ALU.mult).then_inc(neg_max, 1)

            def sums(g, par):
                dve.wait_ge(exp_done, g + 1)
                dve.tensor_tensor(rowsum[:, par:par + 1], expsum[:, par, 0:1], expsum[:, par, 1:2], ALU.add
                                  ).then_inc(sum_done, 1)
                dve.wait_ge(sum_done, g + 1)
                dve.reciprocal(rinv[:, par:par + 1], rowsum[:, par:par + 1]).then_inc(rinv_ready, 1)

            def o_finish(g, par):
                dve.wait_ge(rinv_ready, g + 1)
                dve.wait_ge(olo_ready, g + 1)
                dve.scalar_tensor_tensor(out=o_sb[:], in0=ps[:, ACC, 0:D], scalar=rinv[:, par:par + 1], in1=o_lo[:],
                                         op0=ALU.mult, op1=ALU.add).then_inc(o_ready, 1)

            def heads_high(b, t, g):
                dve.wait_ge(vp_filled, g + 1)
                dve.tensor_copy(headsT[DH:P, t, bass.ds(b * SQ, SQ)], ps[DH:P, MISC, DH:P]).then_inc(vp_high, 1)

            dve.wait_ge(qbd_zeroed, 2)
            for t in range(3):
                q_copy(t)
            for i in range(NCT):
                ct_lo(0, i)
                if i == 5:
                    qp_split_lo(0)
                if i % 2 and i < 6:
                    q_copy(i // 2 + 3)
            max_first(0, 0)
            max_last(0, 0)
            qp_split_lo(1)
            for t in range(6, NT):
                q_copy(t)
            sums(0, 0)

            def step(b, t, first, last):
                g = b * NT + t
                before = not (first and t == 0)
                pb, pt = (b, t - 1) if t else (b - 1, NT - 1)
                if last and t == 1:
                    dve.wait_ge(rows_loaded, 16 * 4)
                if last and 1 <= t <= NI:
                    dve.tensor_tensor(xs[:, t - 1, :], xs[:, t - 1, :], bo_row[:], ALU.add).then_inc(xb_ready, 1)
                if before:
                    o_finish(g - 1, (t + 1) % 2)
                ct = t == CT_STEP and not last
                spread = t == NT - 1 and not last
                more = not (last and t == NT - 1)
                par = (t + 1) % 2
                if spread:
                    for i in range(CT_EARLY, NCT):
                        ct_lo(b + 1, i)
                    max_first(g + 1, par)
                    t_lo(b, t, 0, last)
                    max_last(g + 1, par)
                    t_lo(b, t, 1, last)
                    heads_high(pb, pt, g - 1)
                    t_lo(b, t, 2, last)
                else:
                    for i in range(3):
                        t_lo(b, t, i, last)
                    if more:
                        max_first(g + 1, par)
                    t_lo(b, t, 3, last)
                    if before:
                        heads_high(pb, pt, g - 1)
                    if more:
                        max_last(g + 1, par)
                for i in range(2 if ct else 0):
                    ct_lo(b + 1, i)
                if more:
                    sums(g + 1, par)
                if not (last and t >= NT - 2):
                    qp_split_lo(g + 2)
                for i in range(2, CT_EARLY if ct else 0):
                    ct_lo(b + 1, i)
                if spread:
                    t_lo(b, t, 3, last)

            batches(dve, step)
            o_finish(G - 1, (NT - 1) % 2)

            def wt_split_lo(n):
                dve.wait_ge(wt_hi, n + 1)
                dve.tensor_tensor(wt_dest(n, 1), ps[:, wt_bank(n), :], wt_dest(n, 0).bitcast(F32), ALU.subtract
                                  ).then_inc(wt_ready, 1)

            def add_bias(n, bias, i):
                dve.tensor_tensor(xs[:, i, :], xs[:, i, :], bias[:], ALU.add).then_inc(xb_ready, 1)

            def add_y(n, i):
                dve.wait_ge(y_filled, NI * n + i + 1)
                dve.tensor_tensor(xs[:, i, :], ps[:, Y_BANK[n][i], 0:D], xs[:, i, :], ALU.add).then_inc(x_ready, 1)

            def wts(*ns):
                for n in ns:
                    wt_split_lo(n)

            dve.wait_ge(hp_hi, 1)
            dve.tensor_tensor(headsP[1][:, :, 0:P], headsT[:, :, 0:P], headsP[0][:, :, 0:P].bitcast(F32), ALU.subtract
                              ).then_inc(hp_ready, 1)
            wts(0, 1)
            heads_high(NB - 1, NT - 1, G - 1)
            wts(2, 3)
            dve.wait_ge(xb_ready, NI)
            add_y(0, 0)
            ln_first(1, 0)
            wts(4)
            ln_last(1, 0)
            wts(5, 6)
            add_y(0, 1)
            ln_first(1, 1)
            wts(7)
            ln_last(1, 1)
            wts(8, 9)
            add_y(0, 2)
            xnT_split_lo(1, 0)
            ln_first(1, 2)
            wts(10)
            ln_last(1, 2)
            wts(11)
            add_y(0, 3)
            ln_first(1, 3)
            ln_last(1, 3)

            def soft_shift(i):
                bank = SELF_BANK[i]
                sc = ps[:, bank:bank + 2, :].rearrange("p c (h q) -> p (c h) q", q=SQ)
                dve.wait_ge(s_filled, i + 1)
                dve.tensor_reduce(colmax[:, i % 2, :], sc, AX.X, ALU.max).then_inc(col_max, 1)
                dve.wait_ge(col_max, i + 1)
                if i >= 2:
                    dve.wait_ge(c_filled, 4 * (i - 1))
                dve.tensor_tensor(att[:, i % 2, :, :], sc, colmax[:, i % 2, :].unsqueeze(2).broadcast_to([P, 2 * NT, SQ]),
                                  ALU.subtract).then_inc(s_shifted, 1)

            def soft_norm(i):
                dve.wait_ge(s_exp, i + 1)
                dve.tensor_reduce(colsum[:, i % 2, :], att[:, i % 2, :, :], AX.X, ALU.add).then_inc(col_sum, 1)
                dve.wait_ge(col_sum, i + 1)
                dve.reciprocal(colinv[:, i % 2, :], colsum[:, i % 2, :]).then_inc(col_inv, 1)
                dve.wait_ge(col_inv, i + 1)
                dve.tensor_tensor(att[:, i % 2, :, :], att[:, i % 2, :, :],
                                  colinv[:, i % 2, :].unsqueeze(2).broadcast_to([P, 2 * NT, SQ]), ALU.mult).then_inc(att_ready, 1)

            def heads2_lo(i):
                for c in range(4):
                    dve.wait_ge(c_hi, 4 * i + c + 1)
                    for half in range(2):
                        dst, src = heads2_piece(i, c, half, 1)
                        ins = dve.tensor_tensor(dst, src, heads2_piece(i, c, half, 0)[0].bitcast(F32), ALU.subtract)
                    ins.then_inc(c_ready, 1)

            dve.wait_ge(vb_loaded, 16)
            for u, (kind, h, n) in enumerate(PROJ):
                if kind == "v":
                    if h == 0 and n == 2:
                        xnT_split_lo(1, 1)
                    if h == 1 and n == 0:
                        soft_shift(0)
                        soft_shift(1)
                    i, c = 2 * h + n // 2, n % 2
                    dve.wait_ge(p_filled, u + 1)
                    dve.tensor_tensor(v2[:, i, c * 512:(c + 1) * 512], ps[:, proj_bank(u), :],
                                      vb_row[:, c * 512:(c + 1) * 512], ALU.add).then_inc(p_dve, 1)
                if kind == "q":
                    if h == 0 and n == 0:
                        dve.wait_ge(q2_zeroed, 2)
                    dve.wait_ge(p_filled, u + 1)
                    dve.tensor_scalar(q2[DH:P, n, 4 * h:4 * h + 4, DH:P],
                                      ps[DH:P, proj_bank(u), 0:HT].rearrange("p (b q) -> p b q", q=SQ),
                                      qb_col[DH:P, n:n + 1], None, ALU.add).then_inc(p_dve, 1)
                if kind == "k" and h == 0 and n % 2 == 0:
                    add_bias(1, lb_row, n // 2)
                if wt_after(u) is not None:
                    wt_split_lo(wt_after(u))
                if kind == "q" and h == 1 and n == 3:
                    soft_norm(0)
            soft_norm(1)
            heads2_lo(0)
            heads2_lo(1)
            dve.wait_ge(xb_ready, 2 * NI)
            soft_shift(2)
            soft_shift(3)
            soft_norm(2)
            soft_norm(3)
            add_y(1, 0)
            add_y(1, 1)
            heads2_lo(2)
            ln_first(2, 0)
            ln_first(2, 1)
            ln_last(2, 0)
            ln_last(2, 1)
            heads2_lo(3)
            xnT_split_lo(2, 0)
            for i in range(2, NI):
                add_y(1, i)
                ln_first(2, i)
            for i in range(2, NI):
                ln_last(2, i)
            def h_make(u):
                bank = proj_bank(u)
                dve.wait_ge(g_sig, u + 1)
                dve.tensor_tensor(gs[:, u % 2, :], ps[:, bank, 0:HT], sg[:, u % 2, :], ALU.mult).then_inc(g_silu, 1)
                dve.wait_ge(g_silu, u + 1)
                dve.tensor_tensor(hf[:, u % 2, :], ps[:, bank, HT:2 * HT], gs[:, u % 2, :], ALU.mult).then_inc(h_full, 1)

            def h_split_lo(u):
                m, h = u % NM, u // NM
                dve.wait_ge(h_hi, u + 1)
                dve.tensor_tensor(hTp[:, 1, m, h * HT:(h + 1) * HT], hf[:, u % 2, :],
                                  hTp[:, 0, m, h * HT:(h + 1) * HT].bitcast(F32), ALU.subtract).then_inc(h_ready, 1)

            h_make(0)
            xnT_split_lo(2, 1)
            for u in range(FFN_N):
                if 0 < u < FFN_N - 1:
                    h_make(u + 1)
                h_split_lo(u)
                if u == 0:
                    h_make(1)
                if u == NM:
                    add_y(2, 0)
                    add_y(2, 1)
            add_y(2, 2)
            add_y(2, 3)

        @block.tensor
        def _(pe):
            def product(out, n, left, right):
                for k in range(n):
                    for a, c in ((0, 0), (0, 1), (1, 0)):
                        ins = pe.matmul(out, left(a, k), right(c, k), start=(k == 0 and a + c == 0),
                                        stop=(k == n - 1 and a == 1))
                return ins

            def transpose_xn(n, i):
                pe.wait_ge(ln_done, NI * n + i + 1)
                for k in range(KD):
                    ins = pe.transpose(ps[:, XT[n] + i // 2, k * HT + (i % 2) * P:k * HT + (i % 2 + 1) * P],
                                       xn[:, i, k * P:(k + 1) * P], ident[:])
                if i % 2:
                    ins.then_inc(xnT_filled, 1)

            pe.wait_ge(ident_ready, 1)
            def wk_transposes(c):
                pe.wait_ge(wk_loaded[c], 16)
                for t in range(2 * c, 2 * c + 2):
                    for k in range(KD):
                        col = (t % 2) * D + k * P
                        ins = pe.transpose(ps[:, SC + c, col:col + P], WKs[:, k, t * P:(t + 1) * P], ident[:])
                ins.then_inc(wkT_filled, 1)

            wk_transposes(0)
            wk_transposes(1)
            for i in range(NI):
                transpose_xn(0, i)
            wk_transposes(2)
            wk_transposes(3)
            def project_q(t):
                if t < 4:
                    pe.wait_ge(wkT_copied, t + 1)
                elif t < 6:
                    pe.wait_ge(q_low, t - 3)
                    pe.wait_ge(q_high, t - 3)
                pe.wait_ge(wq_ready, t // 2 + 1)
                cols = [(h * HT, (h + 1) * HT) for h in range(2)] if t == 0 else [(0, TOK)]
                for h, (c0, c1) in enumerate(cols):
                    if t == 0:
                        pe.wait_ge(xnT_ready, h + 1)
                    ins = product(ps[:, QB[t], c0:c1], KD, lambda a, k: WQp[:, a, k, t * P:(t + 1) * P],
                                  lambda a, k: xnT[:, a, k, c0:c1])
                ins.then_inc(q_filled, 1)

            def ctx_transposes(b, i):
                j0, j1 = CTG[i]
                n = ct_base(b) + i
                if not (isinstance(b, int) and b == 0 and i < 2):
                    pe.wait_ge(ring_freed, n - 1)
                for k in range(KD):
                    for j in range(j0, j1):
                        r = P if j < JF else JR
                        c = k * 2 * P + (j - j0) * P
                        ins = pe.transpose(ps[:, ring_bank(i), c:c + r], raw[0:r, j, k * P:(k + 1) * P],
                                           ident[0:r, 0:r])
                ins.then_inc(ring_filled, 1)

            def probs_transposes(b, t, i, last):
                j0, j1 = GROUPS[i]
                pe.wait_ge(ring_freed, t_base(b, t, last) + i - 1)
                for j in range(j0, j1):
                    r = P if j < JF else JR
                    c = (j - j0) * P
                    ins = pe.transpose(ps[0:r, ring_bank(i), c:c + P], probs[:, t % 2, j * P:j * P + r], ident[:])
                ins.then_inc(ring_filled, 1)

            def q_by_wk(b, t, g):
                for k in range(KD):
                    ins = pe.matmul(ps[:, MISC, k * P:(k + 1) * P], WKT[:, t, k * P:(k + 1) * P], qbd[:, t, b, :],
                                    start=True, stop=True)
                ins.then_inc(qp_filled, 1)

            def scores_chunk(n):
                order = [(k, a, c) for k in range(KD) for a, c in ((0, 0), (0, 1), (1, 0))]
                w = CW if n < NC - 1 else CW + 2
                for r, (k, a, c) in enumerate(order):
                    ins = pe.matmul(ps[:, SC + n, 0:w], qp[:, a, k, :], ctxT[:, c, k, n * CW:n * CW + w],
                                    start=(r == 0), stop=(r == len(order) - 1))
                if n >= NC - 2:
                    ins.then_inc(scores_filled, 1)

            def o_transposes(g):
                pe.wait_ge(o_ready, g + 1)
                for k in range(KD):
                    ins = pe.transpose(ps[:, MISC, k * P:(k + 1) * P], o_sb[:, k * P:(k + 1) * P], ident[:])
                ins.then_inc(ot_filled, 1)

            def by_wv(t, g):
                pe.wait_ge(ot_copied, g + 1)
                for k in range(KD):
                    ins = pe.matmul(ps[:, MISC, 0:P], WVs[:, k, t * P:(t + 1) * P], oT[:, k, :],
                                    start=(k == 0), stop=(k == KD - 1))
                ins.then_inc(vp_filled, 1)

            for t in range(3):
                project_q(t)
            pe.wait_ge(raw_loaded, 32)
            for i in range(NCT):
                ctx_transposes(0, i)
                if i % 2 and i < 6:
                    project_q(i // 2 + 3)
                if i == 4:
                    pe.wait_ge(q_low, 1)
                    pe.wait_ge(q_high, 1)
                    q_by_wk(0, 0, 0)
            pe.wait_ge(pads_zeroed, 1)
            pe.wait_ge(qp_ready, 1)
            for n in range(NC):
                if n < 2:
                    pe.wait_ge(q_low, 5 + n)
                    pe.wait_ge(q_high, 5 + n)
                pe.wait_ge(ring_freed, CT_NEED[n])
                scores_chunk(n)
            q_by_wk(0, 1, 1)
            for t in range(6, NT):
                project_q(t)
            pe.wait_ge(wv_loaded, 16)

            def step(b, t, first, last):
                g = b * NT + t
                before = not (first and t == 0)
                after = not (last and t == NT - 1)
                ct = t == CT_STEP and not last
                pt = t - 1 if t else NT - 1
                spread = t == NT - 1 and not last
                pe.wait_ge(exp_done, g + 1)
                if after:
                    pe.wait_ge(qp_ready, g + 2)
                for n in range(NC):
                    if first and t == 0 and n == 1:
                        pe.wait_ge(q_low, NT)
                        pe.wait_ge(q_high, NT)
                    if not spread:
                        probs_transposes(b, t, n, last)
                    elif n == NC - 1:
                        probs_transposes(b, t, 0, last)
                    if n == 2 and before and not spread:
                        pe.wait_ge(qp_ready, g + 2 if after else g + 1)
                        o_transposes(g - 1)
                    if spread:
                        pe.wait_ge(ring_freed, ct_base(b + 1) + CT_NEED[n])
                    if after:
                        scores_chunk(n)
                    if spread and n < NC - 1:
                        ctx_transposes(b + 1, CT_EARLY + n)
                    if spread and n == NC - 2:
                        o_transposes(g - 1)
                if spread:
                    probs_transposes(b, t, 1, last)
                if before:
                    by_wv(pt, g - 1)
                if before:
                    pe.wait_ge(o_ready, g)
                pe.wait_ge(ctx_ready, b + 1)
                for j in range(NJ):
                    if ct and j in CT_AT:
                        if j == 0:
                            pe.wait_ge(raw_loaded, 32 * b + 64)
                        ctx_transposes(b + 1, CT_AT.index(j))
                    if spread and j in (1, 5):
                        probs_transposes(b, t, 2 + j // 5, last)
                    r = P if j < JF else JR
                    for i, (j0, j1) in enumerate(GROUPS):
                        if j == j0:
                            pe.wait_ge(ring_freed, t_base(b, t, last) + i + 1)
                    pe.matmul(ps[:, ACC, :], probsT[0:r, 0, j, :],
                              ctxs[0:r, b % 2, j, :, :].rearrange("p a d -> p (a d)"), start=(j == 0), stop=False)
                    ins = pe.matmul(ps[:, ACC, 0:D], probsT[0:r, 1, j, :], ctxs[0:r, b % 2, j, 0, :],
                                    start=False, stop=(j == NJ - 1))
                    if j == 4 and not (last and t >= NT - 2):
                        nb, nt = (b, t + 2) if t < NT - 2 else (b + 1, t + 2 - NT)
                        if before:
                            pe.wait_ge(vp_low, g)
                            pe.wait_ge(vp_high, g)
                        else:
                            pe.wait_ge(qp_ready, g + 2)
                        q_by_wk(nb, nt, g + 2)
                ins.then_inc(av_filled, 1)

            batches(pe, step)
            def weight_transposes(n, pieces):
                if n >= 8:
                    pe.wait_ge(wt_ready, n - 3)
                for c, piece in enumerate(pieces):
                    ins = pe.transpose(ps[:, wt_bank(n), c * P:(c + 1) * P], piece, ident[:])
                ins.then_inc(wt_filled, 1)

            pe.wait_ge(nat_loaded, 48)

            def attention_weights(n):
                w, c = n // 4, n % 4
                rows = NT if w < 3 else KD
                weight_transposes(n, [nat[w][:, r % rows, (r // rows) * P:(r // rows + 1) * P]
                                      for r in range(4 * c, 4 * c + 4)])

            def ffn_weights(n):
                w, c = (n - 16) // 3, (n - 16) % 3
                rows = NM if w < 2 else KD
                weight_transposes(n, [fnat[w][:, r % rows, (r // rows) * P:(r // rows + 1) * P]
                                      for r in range(4 * c, 4 * c + 4)])

            def project(src, w, i, bank):
                product(ps[:, bank, 0:D], NT, lambda a, t: src[a][:, t, i * P:(i + 1) * P],
                        lambda a, t: w[:, a, t, :]).then_inc(y_filled, 1)

            def project_heads(i):
                pe.wait_ge(hp_ready, i + 1)
                pe.wait_ge(wt_ready, i + 1)
                project(headsP, WOp, i, Y_BANK[0][i])

            for n in range(3):
                attention_weights(n)
            pe.wait_ge(vp_low, G - 1)
            pe.wait_ge(vp_high, G - 1)
            o_transposes(G - 1)
            attention_weights(3)
            pe.wait_ge(ring_freed, t_base(NB - 1, NT - 1, True) + NG)
            attention_weights(4)
            by_wv(NT - 1, G - 1)
            for n in range(5, 7):
                attention_weights(n)
            pe.wait_ge(wo_ready, 1)
            project_heads(0)
            pe.wait_ge(vp_low, G)
            pe.wait_ge(vp_high, G)
            project_heads(1)
            for n in range(7, 10):
                attention_weights(n)
            project_heads(2)
            transpose_xn(1, 0)
            transpose_xn(1, 1)
            for n in range(10, 12):
                attention_weights(n)
            project_heads(3)
            pe.wait_ge(wt_ready, 11)
            pe.wait_ge(xnT_ready, 3)

            def projection(u):
                kind, h, n = PROJ[u]
                if u >= 4:
                    if PROJ[u - 4][0] in "vq":
                        pe.wait_ge(p_dve, dve_done(u - 4))
                    if PROJ[u - 4][0] in "qk":
                        pe.wait_ge(p_act, act_done(u - 4))
                elif u < 2:
                    pe.wait_ge(x_ready, u + 3)
                    if u:
                        pe.wait_ge(wt_ready, 12)
                elif u == 3:
                    pe.wait_ge(xnT_ready, 4)
                bank = proj_bank(u)
                if kind == "v":
                    i = 2 * h + n // 2
                    ins = product(ps[:, bank, :], KD, lambda a, k: xnT[:, a, k, i * P:(i + 1) * P],
                                  lambda a, k: wp[2][:, a, k, (n % 2) * 512:(n % 2 + 1) * 512])
                else:
                    w = wp[0 if kind == "q" else 1]
                    ins = product(ps[:, bank, 0:HT], KD, lambda a, k: w[:, a, k, n * P:(n + 1) * P],
                                  lambda a, k: xnT[:, a, k, h * HT:(h + 1) * HT])
                ins.then_inc(p_filled, 1)
                if u == 1:
                    transpose_xn(1, 2)
                    transpose_xn(1, 3)
                w = wt_after(u)
                if w is not None:
                    if w == 12:
                        pe.wait_ge(nat3_loaded, 16)
                    if w == 16:
                        pe.wait_ge(f_scaled, 3)
                        pe.wait_ge(s_shifted, 2)
                    if w < 16:
                        attention_weights(w)
                    else:
                        ffn_weights(w)

            def self_scores(i):
                for e in range(2):
                    lo = e * SQ
                    for t in range(NT):
                        bank = SELF_BANK[i] + t // 4
                        if i + e == 0 and t == NT - 1:
                            pe.wait_ge(p_act, act_done(len(PROJ) // 2 - 1))
                        ins = pe.matmul(ps[lo:lo + SQ, bank, (t % 4) * P:(t % 4 + 1) * P],
                                        kT2[:, t, i * P + lo:i * P + lo + SQ], q2[:, t, 2 * i + e, :],
                                        start=True, stop=True)
                ins.then_inc(s_filled, 1)

            def self_heads(i):
                pe.wait_ge(att_ready, i + 1)
                for c in range(4):
                    e, t0 = c // 2, (c % 2) * 4
                    lo = e * SQ
                    if i == 0 and c == 2:
                        pe.wait_ge(p_act, act_done(len(PROJ) - 1))
                    for t in range(t0, t0 + 4):
                        ins = pe.matmul(ps[:, HEAD_BANKS[i][c], (t - t0) * P:(t - t0 + 1) * P],
                                        v2[lo:lo + SQ, i, t * P:(t + 1) * P],
                                        att[lo:lo + SQ, i % 2, 2 * t:2 * t + 2, :].rearrange("p h q -> p (h q)"),
                                        start=True, stop=True)
                    ins.then_inc(c_filled, 1)

            def project_self(i):
                project([heads2[:, a, :, :] for a in range(2)], wp[3], i, Y_BANK[1][i])

            half = len(PROJ) // 2
            for u in range(half):
                projection(u)
            pe.wait_ge(wt_ready, 16)
            pe.wait_ge(p_dve, dve_done(half - 1))
            pe.wait_ge(p_act, act_done(half - 2))
            self_scores(0)
            self_scores(1)
            for u in range(half, len(PROJ)):
                projection(u)
            pe.wait_ge(p_dve, dve_done(len(PROJ) - 1))
            pe.wait_ge(p_act, act_done(len(PROJ) - 3))
            self_heads(0)
            pe.wait_ge(wt_ready, WT_N)
            self_heads(1)
            pe.wait_ge(c_ready, 4)
            self_scores(2)
            self_scores(3)
            pe.wait_ge(c_ready, 8)
            project_self(0)
            project_self(1)
            pe.wait_ge(s_shifted, 3)
            self_heads(2)
            pe.wait_ge(s_shifted, 4)
            pe.wait_ge(x_ready, NI + 2)
            self_heads(3)
            pe.wait_ge(c_ready, 12)
            project_self(2)
            transpose_xn(2, 0)
            transpose_xn(2, 1)
            pe.wait_ge(c_ready, 16)
            project_self(3)

            def gate_up(u):
                h, m = u // NM, u % NM
                if u >= 4:
                    pe.wait_ge(h_full, u - 3)
                elif u == 3:
                    pe.wait_ge(xnT_ready, 6)
                for w in range(2):
                    ins = product(ps[:, proj_bank(u), w * HT:(w + 1) * HT], KD,
                                  lambda a, k: fp[w][:, a, k, m * P:(m + 1) * P],
                                  lambda a, k: xnT[:, a, k, h * HT:(h + 1) * HT])
                ins.then_inc(g_filled, 1)

            def down(u):
                h, m = u // NM, u % NM
                pe.wait_ge(h_ready, u + 1)
                if u == NM:
                    pe.wait_ge(x_ready, 2 * NI)
                for i in range(2 * h, 2 * h + 2):
                    for a, c in ((0, 0), (0, 1), (1, 0)):
                        ins = pe.matmul(ps[:, Y_BANK[2][i], 0:D], hTp[:, a, m, i * P:(i + 1) * P], fp[2][:, c, m, :],
                                        start=(m == 0 and a + c == 0), stop=(m == NM - 1 and a == 1))
                    if m == NM - 1:
                        ins.then_inc(y_filled, 1)

            pe.wait_ge(xnT_ready, 5)
            gate_up(0)
            gate_up(1)
            transpose_xn(2, 2)
            transpose_xn(2, 3)
            gate_up(2)
            gate_up(3)
            for u in range(FFN_N):
                down(u)
                if u + 4 < FFN_N:
                    gate_up(u + 4)


_INS = ['x', 'ctx_1024', 'L0_xattn_WQ', 'L0_xattn_WK', 'L0_xattn_WV', 'L0_xattn_WO', 'L0_xattn_bO',
        'L0_attn_q_w', 'L0_attn_q_b', 'L0_attn_k_w', 'L0_attn_k_b', 'L0_attn_v_w', 'L0_attn_v_b',
        'L0_attn_l_w', 'L0_attn_l_b', 'L0_ffn_w_gate', 'L0_ffn_w_up', 'L0_ffn_w_down']
_OUTS = [((8, 64, 256), 'float32')]


def kernel(**inputs):
    import numpy as _np
    import concourse.bacc as _bacc
    from concourse import mybir as _mybir
    from concourse.bass_utils import run_bass_kernel_spmd as _run

    nc = _bacc.Bacc("TRN2", target_bir_lowering=False, num_devices=1)
    arrays, args = {}, []
    for name in _INS:
        a = _np.ascontiguousarray(inputs[name])
        arrays[f"in_{name}_dram"] = a
        args.append(nc.dram_tensor(f"in_{name}_dram", a.shape, _mybir.dt.from_np(a.dtype), kind="ExternalInput").ap())
    for i, (shape, dtype) in enumerate(_OUTS):
        dt = _mybir.dt.from_np(_np.dtype(dtype))
        args.append(nc.dram_tensor(f"out_{i}_dram", shape, dt, kind="ExternalOutput").ap())
    perceiver_layer(nc, *args)
    r = _run(nc, [arrays], core_ids=[0])
    return r.results[0]["out_0_dram"]
```
